# Optimizing a Trainium2 kernel written in Bass

```python
import numpy as np
import jax
import jax.numpy as jnp

def _softmax(x, axis=-1):
    return jax.nn.softmax(x, axis=axis)

def _gelu(x):
    return jax.nn.gelu(x, approximate=True)

def _silu(x):
    return jax.nn.silu(x)

def _sigmoid(x):
    return jax.nn.sigmoid(x)

def _layernorm(x, axis=-1, eps=1e-05):
    m = jnp.mean(x, axis=axis, keepdims=True)
    v = jnp.var(x, axis=axis, keepdims=True)
    return (x - m) / jnp.sqrt(v + eps)

def _scatter_add(tgt, idx, src, axis=0):
    return tgt.at[idx].add(src)

def _segment_sum(src, seg, n):
    return jax.ops.segment_sum(src, seg, n)
kernel_name = 'mk_xattn_ffn_d1_seqx_r8_eb4c59'

def setup_inputs(seed: int=0):
    np.random.seed(seed)
    _w = jnp.asarray

    def _rec_inputs():
        import jax
        import jax.numpy as jnp
        _rk = jax.random.key(seed)
        x = 7.22e-05 + 1 * jax.random.normal(jax.random.fold_in(_rk, 1), (8, 128, 512), jnp.float32)
        _lenS = 128 - jax.random.randint(jax.random.fold_in(_rk, 7), (8,), 0, max(1, 128 // 4) + 1, jnp.int32)
        _lenS2 = 128 - jax.random.randint(jax.random.fold_in(_rk, 8), (8,), 0, max(1, 128 // 4) + 1, jnp.int32)
        _ctx_4096P = jax.random.normal(jax.random.fold_in(_rk, 11), (8, 16, 512), jnp.float32)
        _ctx_4096c = jax.random.dirichlet(jax.random.fold_in(_rk, 511), 0.3 * jnp.ones((16,), jnp.float32), (8, 128))
        _ctx_4096t = jnp.einsum('bsk,bkd->bsd', _ctx_4096c, _ctx_4096P)
        _ctx_4096t = _ctx_4096t * jax.lax.rsqrt(jnp.mean(jnp.square(_ctx_4096t)) + 1e-12) * 0.953939
        ctx_4096 = 4.13588e-05 + 0.999923 * (_ctx_4096t + 0.3 * jax.random.normal(jax.random.fold_in(_rk, 611), (8, 128, 512), jnp.float32))
        _validS = jnp.arange(128)[None, :] < _lenS[:, None]
        _validS2 = jnp.arange(128)[None, :] < _lenS2[:, None]
        _causal = jnp.tril(jnp.ones((128, 128), dtype=bool))
        mask_BxSxS2_bk0 = jnp.logical_not(jnp.broadcast_to(_validS2[:, None, :], (8, 128, 128)))
        return (x, ctx_4096, mask_BxSxS2_bk0)
    x, ctx_4096, mask_BxSxS2_bk0 = _rec_inputs()

    def _L0_xattn_setup():
        import jax, jax.numpy as jnp
        import numpy as np
        B, LQ, LK, D, H, DH = (2, 128, 128, 512, 32, 128)
        EPS = 1e-05

        def _rmsnorm(x, weight):
            var = jnp.mean(jnp.square(x), axis=-1, keepdims=True)
            return x * jax.lax.rsqrt(var + EPS) * weight
        key = jax.random.key(seed)
        ks = jax.random.split(key, 8)
        scale = 0.02
        return {'hidden_states': jax.random.normal(ks[0], (B, LQ, D), jnp.float32), 'key_value_states': jax.random.normal(ks[1], (B, LK, D), jnp.float32), 'attention_mask': jax.random.randint(ks[2], (B, LQ, LK), 0, 2) > 0, 'position_bias': jax.random.normal(ks[3], (H, LQ, LK), jnp.float32), 'ln_weight': jnp.ones((D,), jnp.float32), 'w_q': jax.random.normal(ks[4], (H * DH, D), jnp.float32) * scale, 'w_k': jax.random.normal(ks[5], (H * DH, D), jnp.float32) * scale, 'w_v': jax.random.normal(ks[6], (H * DH, D), jnp.float32) * scale, 'w_out': jax.random.normal(ks[7], (D, H * DH), jnp.float32) * scale}
    _L0_xattn_all = _L0_xattn_setup()
    _L0_xattn_in = {k: v for k, v in _L0_xattn_all.items() if k in ('position_bias', 'ln_weight', 'w_q', 'w_k', 'w_v', 'w_out')}
    del _L0_xattn_all

    def _L0_ffn_setup():
        import jax, jax.numpy as jnp
        import numpy as np
        NF4_CODE = jnp.array([-1.0, -0.6961928009986877, -0.5250730514526367, -0.39491748809814453, -0.28444138169288635, -0.18477343022823334, -0.09105003625154495, 0.0, 0.07958029955625534, 0.16093020141124725, 0.24611230194568634, 0.33791524171829224, 0.44070982933044434, 0.5626170039176941, 0.7229568362236023, 1.0], dtype=jnp.float32)
        SCALE = 32.0 / 16.0
        key = jax.random.key(seed)
        k1, k2, k3, k4, k5 = jax.random.split(key, 5)
        B, S, IN, OUT, R = (4, 256, 512, 512, 16)
        BLK = 64
        x = jax.random.normal(k1, (B, S, IN), dtype=jnp.float32)
        w_codes = jax.random.randint(k2, (OUT, IN), 0, 16, dtype=jnp.int32)
        absmax = jax.random.uniform(k3, (OUT, IN // BLK), dtype=jnp.float32)
        W_a = jax.random.normal(k4, (IN, R), dtype=jnp.float32)
        W_b = jax.random.normal(k5, (R, OUT), dtype=jnp.float32)
        return {'x': x, 'w_codes': w_codes, 'absmax': absmax, 'W_a': W_a, 'W_b': W_b}
    _L0_ffn_all = _L0_ffn_setup()
    _L0_ffn_in = {k: v for k, v in _L0_ffn_all.items() if k in ('w_codes', 'absmax', 'W_a', 'W_b')}
    del _L0_ffn_all
    return {'x': x, 'ctx_4096': ctx_4096, 'mask_BxSxS2_bk0': mask_BxSxS2_bk0, 'L0_xattn_position_bias': _L0_xattn_in['position_bias'], 'L0_xattn_ln_weight': _L0_xattn_in['ln_weight'], 'L0_xattn_w_q': _L0_xattn_in['w_q'], 'L0_xattn_w_k': _L0_xattn_in['w_k'], 'L0_xattn_w_v': _L0_xattn_in['w_v'], 'L0_xattn_w_out': _L0_xattn_in['w_out'], 'L0_ffn_w_codes': _L0_ffn_in['w_codes'], 'L0_ffn_absmax': _L0_ffn_in['absmax'], 'L0_ffn_W_a': _L0_ffn_in['W_a'], 'L0_ffn_W_b': _L0_ffn_in['W_b']}

def reference(x, ctx_4096, mask_BxSxS2_bk0, L0_xattn_position_bias, L0_xattn_ln_weight, L0_xattn_w_q, L0_xattn_w_k, L0_xattn_w_v, L0_xattn_w_out, L0_ffn_w_codes, L0_ffn_absmax, L0_ffn_W_a, L0_ffn_W_b):
    import jax
    import jax.numpy as jnp

    def _L0_xattn_ref(hidden_states, key_value_states, attention_mask, position_bias, ln_weight, w_q, w_k, w_v, w_out):
        import jax, jax.numpy as jnp
        import numpy as np
        B, LQ, LK, D, H, DH = (2, 128, 128, 512, 32, 128)
        EPS = 1e-05

        def _rmsnorm(x, weight):
            var = jnp.mean(jnp.square(x), axis=-1, keepdims=True)
            return x * jax.lax.rsqrt(var + EPS) * weight
        x = _rmsnorm(hidden_states, ln_weight)
        b, lq, _ = x.shape
        lk = key_value_states.shape[1]
        h_q = (x @ w_q.T).reshape(b, lq, H, DH)
        h_k = (key_value_states @ w_k.T).reshape(b, lk, H, DH)
        h_v = (key_value_states @ w_v.T).reshape(b, lk, H, DH)
        score = jnp.einsum('bqhd,bkhd->bhqk', h_q, h_k)
        score = score + position_bias[None]
        m = attention_mask[:, None]
        score = jnp.where(m, score, -jnp.inf)
        score = jax.nn.softmax(score, axis=-1)
        score = jnp.where(m, score, 0.0)
        attn = jnp.einsum('bhqk,bkhd->bqhd', score, h_v).reshape(b, lq, H * DH)
        out = attn @ w_out.T
        return hidden_states + out

    def _L0_ffn_ref(x, w_codes, absmax, W_a, W_b):
        import jax, jax.numpy as jnp
        import numpy as np
        NF4_CODE = jnp.array([-1.0, -0.6961928009986877, -0.5250730514526367, -0.39491748809814453, -0.28444138169288635, -0.18477343022823334, -0.09105003625154495, 0.0, 0.07958029955625534, 0.16093020141124725, 0.24611230194568634, 0.33791524171829224, 0.44070982933044434, 0.5626170039176941, 0.7229568362236023, 1.0], dtype=jnp.float32)
        SCALE = 32.0 / 16.0
        out_f, in_f = w_codes.shape
        blocks = absmax.shape[1]
        W = (NF4_CODE[w_codes].reshape(out_f, blocks, -1) * absmax[:, :, None]).reshape(out_f, in_f).astype(x.dtype)
        y = jnp.einsum('bsi,oi->bso', x, W)
        y = y + SCALE * (x @ W_a.astype(x.dtype) @ W_b.astype(x.dtype))
        return y
    x = x + _L0_xattn_ref(_layernorm(x, axis=-1), ctx_4096, mask_BxSxS2_bk0, L0_xattn_position_bias, L0_xattn_ln_weight, L0_xattn_w_q, L0_xattn_w_k, L0_xattn_w_v, L0_xattn_w_out)
    x = x + _L0_ffn_ref(_layernorm(x, axis=-1), L0_ffn_w_codes, L0_ffn_absmax, L0_ffn_W_a, L0_ffn_W_b)
    return x

_drawn_inputs = setup_inputs


def setup_inputs(seed=0):
    import zlib

    import numpy as np

    out = dict(_drawn_inputs(seed))
    spreads = {'L0_xattn_ln_weight': (1.0, 0.2)}
    factors = {'L0_ffn_absmax': 3.028}
    for name, (base, spread) in spreads.items():
        noise = np.random.default_rng([zlib.crc32(name.encode()), seed]).standard_normal(out[name].shape)
        drawn = base * np.exp(spread * noise) if base else spread * noise
        out[name] = jnp.asarray(drawn.astype(out[name].dtype))
    for name, factor in factors.items():
        out[name] = (out[name] * factor).astype(out[name].dtype)
    return out
```

```python
from contextlib import ExitStack

import numpy as np
import concourse.bass as bass
from concourse import mybir

P = 128
B = 8
L = 128
D = 512
C = D // P
H = 32
DH = 128
G = 4
GROUPS = H // G
T = B * L
HT = T // 2
HB = B // 2
R = 16
LORA_SCALE = 32.0 / 16.0
EPS = 1e-5
MASKED = -3e38
QK = 2 * C * DH
OB = D + L
SLICE = C * D // GROUPS
NF4 = (-1.0, -0.6961928009986877, -0.5250730514526367, -0.39491748809814453, -0.28444138169288635,
       -0.18477343022823334, -0.09105003625154495, 0.0, 0.07958029955625534, 0.16093020141124725,
       0.24611230194568634, 0.33791524171829224, 0.44070982933044434, 0.5626170039176941,
       0.7229568362236023, 1.0)

PROJ_FIRST = B + C + 4
PROJ_GROUP = 4 * G + B
PROJ_BANKS = 2
OUT_FIRST = 2 * C
OUT_HEAD = 2 + B
OUT_BANKS = 4

f32 = mybir.dt.float32
f32r = mybir.dt.float32r
bf16 = mybir.dt.bfloat16
i32 = mybir.dt.int32
u8 = mybir.dt.uint8
ALU = mybir.AluOpType
ACT = mybir.ActivationFunctionType
AX = mybir.AxisListType


def halves(h):
    return range(h * HB, (h + 1) * HB)


def xattn_ffn(nc, x_d, ctx_d, mask_d, lnw_d, qk_d, ob_d, wv_d, codes_d, absmax_d, wa_d, wb_d, out_d):
    with ExitStack() as ctx:
        def sb(name, shape, dt=f32):
            return ctx.enter_context(nc.sbuf_tensor(name, shape, dt))

        def sem(name):
            return ctx.enter_context(nc.semaphore(name))

        xn_hi = sb("xn_hi", [P, C, T], f32r)
        xn_lo = sb("xn_lo", [P, C, T], f32r)
        ctx_hi = sb("ctx_hi", [P, C, T], f32r)
        ctx_lo = sb("ctx_lo", [P, C, T], f32r)
        resid = sb("resid", [P, B, D])
        v = sb("v", [P, B, G * DH])
        qT = sb("qT", [P, T])
        kT = sb("kT", [P, T])
        qk_raw = sb("qk_raw", [P, 2, QK])
        qk_hi = sb("qk_hi", [P, 2, QK], f32r)
        qk_lo = sb("qk_lo", [P, 2, QK], f32r)
        ob_raw = sb("ob_raw", [P, 2, OB])
        wo_hi = sb("wo_hi", [P, 2, D], f32r)
        wo_lo = sb("wo_lo", [P, 2, D], f32r)
        wv_raw = sb("wv_raw", [P, C, G * DH])
        wv_hi = sb("wv_hi", [P, C, G * DH], f32r)
        wv_lo = sb("wv_lo", [P, C, G * DH], f32r)
        bias = sb("bias", [P, 2, B, L])
        mask_add = sb("mask_add", [P, B, L], bf16)
        p = sb("p", [P, B, L])
        pT = sb("pT", [P, B, L])
        attn_hi = sb("attn_hi", [P, T], f32r)
        attn_lo = sb("attn_lo", [P, T], f32r)
        w_ffn = sb("w_ffn", [P, C * D])
        codes = sb("codes", [P, SLICE], i32)
        absmax = sb("absmax", [P, SLICE])
        picked = sb("picked", [P, SLICE])
        level = sb("level", [P, SLICE])
        ident = sb("ident", [P, P])
        lnw = sb("lnw", [P, C])
        neg_max = sb("neg_max", [P, B])
        prob_sum = sb("prob_sum", [P, B])
        recip = sb("recip", [P, B])
        row_scale = sb("row_scale", [P, B])
        row_valid = sb("row_valid", [P, B])
        stats = sb("stats", [P, B, 6])
        mean_var = sb("mean_var", [P, B, 2])
        rstd = sb("rstd", [P, B])
        rms_a = sb("rms_a", [P, B])
        rms_b = sb("rms_b", [P, B])
        both = sb("both", [P, B])
        minus_half = sb("minus_half", [P, B])

        ctx_raw = v[:, :, :].rearrange("p b n -> p (b n)").rearrange("p (h c t) -> p h c t", h=2, c=C)
        mask_words = qk_raw[:, 1, 0:B * L // 4].bitcast(i32)
        mask_raw = mask_words.bitcast(u8).rearrange("p (b k) -> p b k", b=B)
        wa = bias[0:R, 1, 0:4, :].rearrange("p b k -> p (b k)")
        wb = bias[0:R, 1, 4:8, :].rearrange("p b k -> p (b k)")

        def stage(b):
            t = (p, pT)[b % 4 // 2]
            return t[:, (b % 2) * 4:(b % 2) * 4 + 4, :].rearrange("p b k -> p (b k)")

        def hidden(b):
            return bias[:, 0, (b % 2) * 4:(b % 2) * 4 + 4, :].rearrange("p b k -> p (b k)")

        proj_ps = [ctx.enter_context(nc.psum_tensor(f"proj_ps{i}", [P, D], f32)) for i in range(PROJ_BANKS)]
        out_ps = [ctx.enter_context(nc.psum_tensor(f"out_ps{i}", [P, D], f32)) for i in range(OUT_BANKS)]
        s_ps = [ctx.enter_context(nc.psum_tensor(f"s_ps{i}", [P, HB, L], f32)) for i in range(2)]

        ctx_loaded = [sem(f"ctx_loaded{i}") for i in range(2)]
        x_loaded = [sem(f"x_loaded{i}") for i in range(2)]
        mask_loaded = sem("mask_loaded")
        small_loaded = sem("small_loaded")
        qk_loaded = [sem(f"qk_loaded{i}") for i in range(2)]
        ob_loaded = [sem(f"ob_loaded{i}") for i in range(2)]
        wv_loaded = sem("wv_loaded")
        codes_loaded = sem("codes_loaded")
        stored = sem("stored")

        ctx_hi_done = sem("ctx_hi_done")
        ctx_lo_done = sem("ctx_lo_done")
        qk_hi_done = sem("qk_hi_done")
        qk_lo_done = sem("qk_lo_done")
        wo_hi_done = sem("wo_hi_done")
        wo_lo_done = sem("wo_lo_done")
        wv_hi_done = sem("wv_hi_done")
        wv_lo_done = sem("wv_lo_done")
        mask_done = sem("mask_done")
        bias_done = sem("bias_done")
        const_done = sem("const_done")

        proj_done = sem("proj_done")
        proj_drained = sem("proj_drained")
        out_done = sem("out_done")
        out_drained = sem("out_drained")
        scores_done = sem("scores_done")
        biased = sem("biased")
        max_done = sem("max_done")
        exp_done = sem("exp_done")
        recip_done = sem("recip_done")
        row_scale_done = sem("row_scale_done")
        p_done = sem("p_done")
        p_read = sem("p_read")
        pT_done = sem("pT_done")
        attn_hi_done = sem("attn_hi_done")

        stats_done = sem("stats_done")
        norm_step = sem("norm_step")
        norm_done = sem("norm_done")
        staged = sem("staged")
        hidden_done = sem("hidden_done")
        hidden_added = sem("hidden_added")
        ident_step = sem("ident_step")
        decode_step = sem("decode_step")
        decoded = sem("decoded")
        pool_passed = sem("pool_passed")

        block = ctx.enter_context(nc.Block())

        @block.sync
        def _(sp):
            def load_qk(h, slot):
                sp.dma_start(qk_raw[:, slot, :], qk_d[h]).then_inc(qk_loaded[slot], 16)

            def load_ob(h, slot):
                sp.dma_start(ob_raw[:, slot, :], ob_d[h]).then_inc(ob_loaded[slot], 16)

            def load_wv(g):
                sp.dma_start(wv_raw[:, :, :].rearrange("p c n -> p (c n)"), wv_d[g]).then_inc(wv_loaded, 16)

            def load_codes(g):
                sp.dma_start(codes[:, :], codes_d[g]).then_inc(codes_loaded, 16)
                for s in range(2):
                    sp.dma_start(absmax[64 * s:64 * s + 64, :],
                                 absmax_d[g, s].partition_broadcast(64)).then_inc(codes_loaded, 16)

            sp.dma_start(ctx_raw[:, 0, :, :], ctx_d[0]).then_inc(ctx_loaded[0], 16)
            load_wv(0)
            for hf in range(2):
                sp.dma_start(resid[:, hf * HB:(hf + 1) * HB, :],
                             x_d[hf * HB:(hf + 1) * HB].rearrange("b t d -> t b d")).then_inc(x_loaded[hf], 16)
                if hf == 0:
                    sp.dma_start(ctx_raw[:, 1, :, :], ctx_d[1]).then_inc(ctx_loaded[1], 16)
                    sp.dma_start(mask_words, mask_d).then_inc(mask_loaded, 16)
            sp.dma_start(lnw[:, :], lnw_d).then_inc(small_loaded, 16)
            sp.dma_start(wa, wa_d).then_inc(small_loaded, 16)
            sp.dma_start(wb, wb_d).then_inc(small_loaded, 16)
            load_qk(0, 0)
            load_ob(0, 0)
            load_ob(1, 1)
            load_codes(0)
            sp.wait_ge(mask_done, 2)
            load_qk(1, 1)
            for h in range(2):
                sp.wait_ge(qk_lo_done, h + 1)
                load_qk(h + 2, h)
            sp.wait_ge(wo_lo_done, 1)
            sp.wait_ge(bias_done, 1)
            load_ob(2, 0)

            def group(g, last):
                if not last:
                    sp.wait_ge(wv_lo_done, C * (g + 1))
                    load_wv(g + 1)
                for j in range(G):
                    h = G * g + j
                    if not (last and j + 4 >= G):
                        sp.wait_ge(qk_lo_done, h + 3)
                        load_qk(h + 4, j % 2)
                    if not (last and j + 3 >= G):
                        sp.wait_ge(wo_lo_done, h + 2)
                        sp.wait_ge(bias_done, h + 2)
                        load_ob(h + 3, (j + 1) % 2)
                if not last:
                    sp.wait_ge(decoded, g + 1)
                    load_codes(g + 1)

            with sp.Fori(0, GROUPS - 1) as g:
                group(g, False)
            group(GROUPS - 1, True)

            for b in range(B):
                sp.wait_ge(out_drained, OUT_BANKS + OUT_FIRST + OUT_HEAD * H + ffn_chain(b, 1) + 1)
                sp.dma_start(out_d[b], resid[:, b, :]).then_inc(stored, 16)
            sp.wait_ge(stored, 16 * B)

        @block.gpsimd
        def _(pool):
            def passed(s, value):
                pool.wait_ge(s, value)
                pool.sem_inc(pool_passed, 1)

            pool.memset(minus_half[:, :], -0.5).then_inc(const_done, 1)
            pool.memset(ident[:, :], 0.0).then_inc(ident_step, 1)
            pool.wait_ge(ident_step, 1)
            pool.affine_select(out=ident[:, :], in_=ident[:, :], compare_op=ALU.not_equal, fill=1.0, base=0,
                               pattern=[[-1, P]], channel_multiplier=1).then_inc(const_done, 1)

            steps = [0]

            def norm(ins):
                ins.then_inc(norm_step, 1)
                steps[0] += 1
                pool.wait_ge(norm_step, steps[0])

            pool.wait_ge(const_done, 2)
            for hf in range(2):
                bs = slice(hf * HB, (hf + 1) * HB)
                var = mean_var[:, bs, 1]
                pool.wait_ge(stats_done, 2 * HB * (hf + 1))
                norm(pool.tensor_scalar(rms_a[:, bs], var, EPS, None, ALU.add))
                norm(pool.tensor_tensor(rstd[:, bs], rms_a[:, bs], minus_half[:, bs], ALU.pow))
                norm(pool.tensor_tensor(rms_a[:, bs], rstd[:, bs], rstd[:, bs], ALU.mult))
                norm(pool.tensor_tensor(rms_b[:, bs], rms_a[:, bs], var, ALU.mult))
                norm(pool.tensor_scalar(rms_a[:, bs], rms_b[:, bs], EPS, None, ALU.add))
                norm(pool.tensor_tensor(rms_b[:, bs], rms_a[:, bs], minus_half[:, bs], ALU.pow))
                pool.tensor_tensor(both[:, bs], rms_b[:, bs], rstd[:, bs], ALU.mult).then_inc(norm_done, 1)

            for b in range(B):
                pool.wait_ge(hidden_done, b + 1)
                pool.tensor_tensor(resid[:, b, :], resid[:, b, :], hidden(b), ALU.add).then_inc(hidden_added, 1)

            def make_bias(slot):
                pos = ob_raw[:, slot, D:OB].rearrange("p (o k) -> p o k", o=1).broadcast_to([P, B, L])
                pool.tensor_tensor(bias[:, slot, :, :], pos, mask_add[:, :, :], ALU.add).then_inc(bias_done, 1)

            pool.wait_ge(mask_done, 2)
            pool.wait_ge(hidden_added, B)
            pool.wait_ge(ob_loaded[0], 16)
            make_bias(0)

            per_slice = 2 * (len(NF4) - 1) + 1

            def decode(g, quarter):
                step = [per_slice * g + (0, 7, 13, 21)[quarter]]

                def then(ins):
                    ins.then_inc(decode_step, 1)
                    step[0] += 1
                    passed(decode_step, step[0])

                if quarter == 0:
                    passed(codes_loaded, 48 * (g + 1))
                for code in range(4 * quarter, 4 * quarter + 4):
                    value = NF4[code]
                    if value == 0.0:
                        continue
                    match = ALU.is_ge if code == len(NF4) - 1 else ALU.is_equal
                    then(pool.tensor_scalar((level if code == 0 else picked)[:, :], codes[:, :], float(code), value,
                                            match, ALU.mult))
                    if code:
                        then(pool.tensor_tensor(level[:, :], level[:, :], picked[:, :], ALU.add))
                if quarter == 3:
                    then(pool.tensor_tensor(picked[:, :], level[:, :], absmax[:, :], ALU.mult))
                    at = bass.ds(g * SLICE, SLICE)
                    then(pool.tensor_tensor(w_ffn[:, at], w_ffn[:, at], picked[:, :], ALU.add))
                    pool.sem_inc(decoded, 1)

            def group(g, last):
                for j in range(G):
                    h = G * g + j
                    passed(p_done, 2 * h + 2)
                    if not (last and j == G - 1):
                        passed(ob_loaded[(j + 1) % 2], 16 * (2 * g + (j + 1) // 2 + 1))
                        make_bias((j + 1) % 2)
                    decode(g, j)

            with pool.Fori(0, GROUPS - 1) as g:
                group(g, False)
            group(GROUPS - 1, True)

            base = 2 * B
            for b in range(B):
                one = slice(b, b + 1)
                pool.wait_ge(stats_done, base + 2 * (b + 1))
                norm(pool.tensor_scalar(rms_a[:, one], mean_var[:, b, 1:2], EPS, None, ALU.add))
                pool.tensor_tensor(rstd[:, one], rms_a[:, one], minus_half[:, one], ALU.pow).then_inc(norm_done, 1)

        @block.scalar
        def _(act):
            def copy(out, in_, **kw):
                return act.activation(out, in_, ACT.Copy, **kw)

            def split_wv(c, source):
                copy(wv_hi[:, c, :], source).then_inc(wv_hi_done, 1)

            act.wait_ge(ctx_loaded[0], 16)
            for c in range(C):
                copy(ctx_hi[:, c, 0:HT], ctx_raw[:, 0, c, :]).then_inc(ctx_hi_done, 1)
            act.wait_ge(wv_loaded, 16)
            for c in range(C):
                split_wv(c, wv_raw[:, c, :])
            act.wait_ge(ctx_loaded[1], 16)
            for c in range(C):
                copy(ctx_hi[:, c, HT:T], ctx_raw[:, 1, c, :]).then_inc(ctx_hi_done, 1)

            def drain(n, bank, out, **kw):
                act.wait_ge(proj_done, n + 1)
                copy(out, proj_ps[bank][:, :], **kw).then_inc(proj_drained, 1)

            for b in range(HB):
                drain(b, b % 2, v[:, b, :])
            act.wait_ge(qk_loaded[0], 16)
            copy(qk_hi[:, 0, :], qk_raw[:, 0, :]).then_inc(qk_hi_done, 1)
            for b in range(HB, B):
                drain(b, b % 2, v[:, b, :])
            for c in range(C):
                drain(B + c, c % 2, w_ffn[:, c * D:(c + 1) * D], scale=LORA_SCALE)
            for hf in range(2):
                drain(B + C + hf, hf, kT[:, hf * HT:(hf + 1) * HT])
            act.wait_ge(qk_loaded[1], 16)
            copy(qk_hi[:, 1, :], qk_raw[:, 1, :]).then_inc(qk_hi_done, 1)

            act.wait_ge(small_loaded, 48)
            for hf in range(2):
                for c in range(C):
                    act.wait_ge(out_done, C * hf + c + 1)
                    copy(xn_hi[:, c, hf * HT:(hf + 1) * HT], out_ps[c][:, :],
                         scale=lnw[:, c:c + 1]).then_inc(attn_hi_done, 1)
            for hf in range(2):
                drain(B + C + 2 + hf, hf, qT[:, hf * HT:(hf + 1) * HT])
            act.wait_ge(ob_loaded[0], 16)
            copy(wo_hi[:, 0, :], ob_raw[:, 0, 0:D]).then_inc(wo_hi_done, 1)
            act.wait_ge(qk_loaded[0], 32)
            copy(qk_hi[:, 0, :], qk_raw[:, 0, :]).then_inc(qk_hi_done, 1)

            def group(g, last):
                for j in range(G):
                    h = G * g + j
                    final = last and j == G - 1
                    n = PROJ_FIRST + PROJ_GROUP * g + 4 * j
                    for hf in range(2):
                        act.wait_ge(max_done, 2 * h + hf + 1)
                        for b in halves(hf):
                            e = act.activation(p[:, b, :], p[:, b, :], ACT.Exp, bias=neg_max[:, b:b + 1],
                                               accum_out=prob_sum[:, b:b + 1])
                        e.then_inc(exp_done, 1)
                    if not final:
                        for hf in range(2):
                            drain(n + hf, hf, qT[:, hf * HT:(hf + 1) * HT])
                        slot = (j + 1) % 2
                        act.wait_ge(ob_loaded[slot], 16 * (2 * g + (j + 1) // 2 + 1))
                        act.wait_ge(out_done, OUT_FIRST + OUT_HEAD * h)
                        copy(wo_hi[:, slot, :], ob_raw[:, slot, 0:D]).then_inc(wo_hi_done, 1)
                        drain(n + 2, 0, kT[:, 0:HT])
                    for hf in range(2):
                        act.wait_ge(out_done, OUT_FIRST + OUT_HEAD * h + hf + 1)
                        copy(attn_hi[:, hf * HT:(hf + 1) * HT],
                             out_ps[(2 * j + hf) % OUT_BANKS][:, :]).then_inc(attn_hi_done, 1)
                    if not final:
                        drain(n + 3, 1, kT[:, HT:T])
                    if not (last and j + 3 >= G):
                        slot = (j + 1) % 2
                        act.wait_ge(qk_loaded[slot], 16 * (2 * g + (j + 3) // 2 + 1))
                        copy(qk_hi[:, slot, :], qk_raw[:, slot, :]).then_inc(qk_hi_done, 1)
                    if not last:
                        if j == 0:
                            act.wait_ge(wv_loaded, 16 * (g + 2))
                        for c in ((0, 1), (2,), (3,), ())[j]:
                            split_wv(c, wv_raw[:, c, :])
                    else:
                        act.wait_ge(decoded, GROUPS if j == G - 1 else GROUPS - 1)
                        split_wv(j, w_ffn[:, j * D:(j + 1) * D])
                    if not last and j == G - 1:
                        for b in range(B):
                            drain(n + 4 + b, b % 2, v[:, b, :])

            with act.Fori(0, GROUPS - 1) as g:
                group(g, False)
            group(GROUPS - 1, True)

            for b in range(B):
                act.wait_ge(out_done, OUT_FIRST + OUT_HEAD * H + ffn_chain(b, 0) + 1)
                copy(xn_hi[:, :, b * L:(b + 1) * L],
                     out_ps[ffn_chain(b, 0) % OUT_BANKS][:, :].rearrange("p (c t) -> p c t", c=C)).then_inc(attn_hi_done, 1)

        @block.vector
        def _(dve):
            def lo(out, whole, hi):
                return dve.tensor_tensor(out, whole, hi.bitcast(f32), ALU.subtract)

            def out_count(h):
                return OUT_FIRST + OUT_HEAD * h

            dve.memset(neg_max[:, :], 0.0).then_inc(out_drained, OUT_BANKS)
            dve.memset(row_scale[:, :], 0.0).then_inc(p_read, 2)
            dve.memset(recip[:, :], 0.0).then_inc(pT_done, 2)

            dve.wait_ge(ctx_loaded[0], 16)
            for c in range(C):
                dve.wait_ge(ctx_hi_done, c + 1)
                lo(ctx_lo[:, c, 0:HT], ctx_raw[:, 0, c, :], ctx_hi[:, c, 0:HT]).then_inc(ctx_lo_done, 1)
            for c in range(C):
                dve.wait_ge(wv_hi_done, c + 1)
                lo(wv_lo[:, c, :], wv_raw[:, c, :], wv_hi[:, c, :]).then_inc(wv_lo_done, 1)

            def tile_stats(b, before):
                dve.bn_stats(stats[:, b, :], resid[:, b, :]).then_inc(stats_done, 1)
                dve.wait_ge(stats_done, before + 1)
                dve.bn_aggr(mean_var[:, b, :], stats[:, b, :]).then_inc(stats_done, 1)

            dve.wait_ge(x_loaded[0], 16)
            for b in halves(0):
                tile_stats(b, 2 * b)
            for c in range(C):
                dve.wait_ge(ctx_hi_done, C + c + 1)
                lo(ctx_lo[:, c, HT:T], ctx_raw[:, 1, c, :], ctx_hi[:, c, HT:T]).then_inc(ctx_lo_done, 1)
            dve.wait_ge(x_loaded[1], 16)
            for b in halves(1):
                tile_stats(b, 2 * b)
            dve.wait_ge(qk_hi_done, 1)
            lo(qk_lo[:, 0, :], qk_raw[:, 0, :], qk_hi[:, 0, :]).then_inc(qk_lo_done, 1)

            dve.wait_ge(mask_loaded, 16)
            dve.tensor_scalar(mask_add[:, :, :], mask_raw, 1.0, -MASKED, ALU.subtract, ALU.mult).then_inc(mask_done, 1)
            dve.tensor_reduce(row_valid[:, :], mask_raw, AX.X, ALU.max).then_inc(mask_done, 1)

            for b in range(B):
                if b % HB == 0:
                    dve.wait_ge(norm_done, b // HB + 1)
                if b == HB:
                    dve.wait_ge(out_done, C)
                dve.tensor_scalar(stage(b), resid[:, b, :], mean_var[:, b, 0:1], both[:, b:b + 1],
                                  ALU.subtract, ALU.mult).then_inc(staged, 1)
                if b >= 2:
                    dve.wait_ge(hidden_added, b - 1)
                dve.tensor_scalar(hidden(b), resid[:, b, :], mean_var[:, b, 0:1], rstd[:, b:b + 1],
                                  ALU.subtract, ALU.mult).then_inc(hidden_done, 1)
                if b % HB == HB - 1:
                    hf = b // HB
                    for c in range(C):
                        dve.wait_ge(attn_hi_done, C * hf + c + 1)
                        dve.scalar_tensor_tensor(
                            xn_lo[:, c, hf * HT:(hf + 1) * HT], out_ps[c][:, :], lnw[:, c:c + 1],
                            xn_hi[:, c, hf * HT:(hf + 1) * HT].bitcast(f32), ALU.mult, ALU.subtract,
                        ).then_inc(out_drained, 1)
            dve.wait_ge(qk_hi_done, 2)
            lo(qk_lo[:, 1, :], qk_raw[:, 1, :], qk_hi[:, 1, :]).then_inc(qk_lo_done, 1)
            dve.wait_ge(wo_hi_done, 1)
            lo(wo_lo[:, 0, :], ob_raw[:, 0, 0:D], wo_hi[:, 0, :]).then_inc(wo_lo_done, 1)

            def group(g, last):
                for j in range(G):
                    h = G * g + j
                    final = last and j == G - 1
                    for hf in range(2):
                        bs = slice(hf * HB, (hf + 1) * HB)
                        dve.wait_ge(scores_done, 2 * h + hf + 1)
                        if hf == 0:
                            dve.wait_ge(bias_done, h + 1)
                            dve.wait_ge(p_read, 2 * h + 2)
                        dve.tensor_tensor(p[:, bs, :], s_ps[hf][:, :, :], bias[:, j % 2, bs, :],
                                          ALU.add).then_inc(biased, 1)
                        dve.wait_ge(biased, 2 * h + hf + 1)
                        dve.tensor_reduce(neg_max[:, bs], p[:, bs, :], AX.X, ALU.max,
                                          negate=True).then_inc(max_done, 1)
                    for hf in range(2):
                        bs = slice(hf * HB, (hf + 1) * HB)
                        dve.wait_ge(exp_done, 2 * h + hf + 1)
                        dve.reciprocal(recip[:, bs], prob_sum[:, bs]).then_inc(recip_done, 1)
                        dve.wait_ge(recip_done, 2 * h + hf + 1)
                        dve.tensor_tensor(row_scale[:, bs], recip[:, bs], row_valid[:, bs],
                                          ALU.mult).then_inc(row_scale_done, 1)
                        dve.wait_ge(row_scale_done, 2 * h + hf + 1)
                        scale = row_scale[:, bs].rearrange("p (b o) -> p b o", o=1).broadcast_to([P, HB, L])
                        dve.tensor_tensor(p[:, bs, :], p[:, bs, :], scale, ALU.mult).then_inc(p_done, 1)
                    if not (last and j + 2 >= G):
                        slot = j % 2
                        dve.wait_ge(qk_hi_done, h + 3)
                        lo(qk_lo[:, slot, :], qk_raw[:, slot, :], qk_hi[:, slot, :]).then_inc(qk_lo_done, 1)
                    if not final:
                        slot = (j + 1) % 2
                        dve.wait_ge(wo_hi_done, h + 2)
                        lo(wo_lo[:, slot, :], ob_raw[:, slot, 0:D], wo_hi[:, slot, :]).then_inc(wo_lo_done, 1)
                    for hf in range(2):
                        dve.wait_ge(p_read, 2 * h + hf + 3)
                        dve.tensor_copy(pT[:, hf * HB:(hf + 1) * HB, :], s_ps[hf][:, :, :]).then_inc(pT_done, 1)
                    for hf in range(2):
                        dve.wait_ge(attn_hi_done, 2 * C + 2 * h + hf + 1)
                        at = slice(hf * HT, (hf + 1) * HT)
                        lo(attn_lo[:, at], out_ps[(2 * j + hf) % OUT_BANKS][:, :],
                           attn_hi[:, at]).then_inc(out_drained, 1)
                    for b in range(B):
                        dve.wait_ge(out_done, out_count(h) + 2 + b + 1)
                        if b == 0:
                            dve.wait_ge(out_drained, OUT_BANKS + out_count(h) + 2)
                        dve.tensor_tensor(resid[:, b, :], out_ps[(2 * j + 2 + b) % OUT_BANKS][:, :],
                                          resid[:, b, :], ALU.add).then_inc(out_drained, 1)
                        if final:
                            dve.wait_ge(out_drained, OUT_BANKS + out_count(h) + 2 + b + 1)
                            tile_stats(b, 2 * B + 2 * b)
                            if 1 <= b < B - 1:
                                ffn_norm(b - 1)
                    if not last:
                        for c in ((0, 1), (2,), (3,), ())[j]:
                            dve.wait_ge(wv_hi_done, C * (g + 1) + c + 1)
                            lo(wv_lo[:, c, :], wv_raw[:, c, :], wv_hi[:, c, :]).then_inc(wv_lo_done, 1)
                    else:
                        dve.wait_ge(wv_hi_done, C * GROUPS + j + 1)
                        lo(wv_lo[:, j, :], w_ffn[:, j * D:(j + 1) * D], wv_hi[:, j, :]).then_inc(wv_lo_done, 1)

            def ffn_norm(b):
                dve.wait_ge(norm_done, 2 + b + 1)
                if b >= 4:
                    dve.wait_ge(out_done, out_count(H) + ffn_chain(b - 4, 0) + 1)
                dve.tensor_scalar(stage(b), resid[:, b, :], mean_var[:, b, 0:1], rstd[:, b:b + 1],
                                  ALU.subtract, ALU.mult).then_inc(staged, 1)

            with dve.Fori(0, GROUPS - 1) as g:
                group(g, False)
            group(GROUPS - 1, True)

            def ffn_lo(b):
                n = ffn_chain(b, 0)
                dve.wait_ge(attn_hi_done, 2 * C + 2 * H + b + 1)
                at = slice(b * L, (b + 1) * L)
                lo(xn_lo[:, :, at], out_ps[n % OUT_BANKS][:, :].rearrange("p (c t) -> p c t", c=C),
                   xn_hi[:, :, at]).then_inc(out_drained, 1)

            ffn_lo(0)
            for b in range(B):
                if b + 1 < B:
                    ffn_lo(b + 1)
                n = ffn_chain(b, 1)
                dve.wait_ge(out_done, out_count(H) + n + 1)
                dve.tensor_tensor(resid[:, b, :], out_ps[n % OUT_BANKS][:, :], resid[:, b, :],
                                  ALU.add).then_inc(out_drained, 1)
                if b < 2:
                    ffn_norm(B - 2 + b)

        @block.tensor
        def _(pe):
            def three(out, pairs, sem_done):
                n = 3 * len(pairs)
                i = 0
                for (l_hi, l_lo), (r_hi, r_lo) in pairs:
                    for l, r in ((l_hi, r_hi), (l_hi, r_lo), (l_lo, r_hi)):
                        m = pe.matmul(out, l, r, start=(i == 0), stop=(i == n - 1))
                        i += 1
                m.then_inc(sem_done, 1)

            def proj_bank(n, bank, first=False):
                if not first:
                    pe.wait_ge(proj_drained, n - PROJ_BANKS + 1)
                return proj_ps[bank][:, :]

            def values(n, b, first=False):
                at = slice(b * L, (b + 1) * L)
                three(proj_bank(n, b % 2, first),
                      [((ctx_hi[:, c, at], ctx_lo[:, c, at]), (wv_hi[:, c, :], wv_lo[:, c, :])) for c in range(C)],
                      proj_done)

            def project(n, slot, which, hf):
                a_hi, a_lo = ((xn_hi, xn_lo), (ctx_hi, ctx_lo))[which]
                at = slice(hf * HT, (hf + 1) * HT)

                def w(t, c):
                    k = (which * C + c) * DH
                    return t[:, slot, k:k + DH]

                three(proj_bank(n, hf),
                      [((w(qk_hi, c), w(qk_lo, c)), (a_hi[:, c, at], a_lo[:, c, at])) for c in range(C)],
                      proj_done)

            def out_bank(n_bank, count):
                pe.wait_ge(out_drained, count)
                return out_ps[n_bank]

            pe.wait_ge(ctx_lo_done, C)
            pe.wait_ge(wv_lo_done, C)
            for b in range(B):
                if b == HB:
                    pe.wait_ge(ctx_lo_done, 2 * C)
                values(b, b, first=b < 2)
            pe.wait_ge(small_loaded, 48)
            for c in range(C):
                pe.matmul(proj_bank(B + c, c % 2), wa[:, c * P:(c + 1) * P], wb, start=True,
                          stop=True).then_inc(proj_done, 1)
            pe.wait_ge(qk_lo_done, 1)
            for hf in range(2):
                project(B + C + hf, 0, 1, hf)

            pe.wait_ge(const_done, 2)
            for hf in range(2):
                pe.wait_ge(staged, HB * (hf + 1))
                for c in range(C):
                    bank = out_bank(c, C * hf + c + 1)
                    for i, b in enumerate(halves(hf)):
                        t = pe.transpose(bank[:, i * P:(i + 1) * P], stage(b)[:, c * P:(c + 1) * P], ident[:, :])
                    t.then_inc(out_done, 1)
                
            pe.wait_ge(out_drained, OUT_BANKS + OUT_FIRST)
            for hf in range(2):
                project(B + C + 2 + hf, 0, 0, hf)

            def group(g, last):
                for j in range(G):
                    h = G * g + j
                    final = last and j == G - 1
                    n = PROJ_FIRST + PROJ_GROUP * g + 4 * j
                    m = OUT_FIRST + OUT_HEAD * h
                    pe.wait_ge(proj_drained, n)
                    pe.wait_ge(pT_done, 2 * h + 2)
                    for hf in range(2):
                        for i, b in enumerate(halves(hf)):
                            at = slice(b * L, (b + 1) * L)
                            s = pe.matmul(s_ps[hf][:, i, :], qT[:, at], kT[:, at], start=True, stop=True)
                        s.then_inc(scores_done, 1)
                    if not final:
                        slot = (j + 1) % 2
                        pe.wait_ge(qk_lo_done, h + 2)
                        project(n, slot, 0, 0)
                        project(n + 1, slot, 0, 1)
                        project(n + 2, slot, 1, 0)
                    for hf in range(2):
                        pe.wait_ge(p_done, 2 * h + hf + 1)
                        for i, b in enumerate(halves(hf)):
                            t = pe.transpose(s_ps[hf][:, i, :], p[:, b, :], ident[:, :])
                        t.then_inc(p_read, 1)
                    for hf in range(2):
                        pe.wait_ge(pT_done, 2 * h + hf + 1 + 2)
                        bank = out_bank((2 * j + hf) % OUT_BANKS, m + hf + 1)
                        for i, b in enumerate(halves(hf)):
                            o = pe.matmul(bank[:, i * L:(i + 1) * L], v[:, b, j * DH:(j + 1) * DH], pT[:, b, :],
                                          start=True, stop=True)
                        o.then_inc(out_done, 1)
                    if not final:
                        project(n + 3, (j + 1) % 2, 1, 1)
                    if not last and j == G - 1:
                        pe.wait_ge(wv_lo_done, C * (g + 2))
                        for b in range(B):
                            values(n + 4 + b, b)
                    pe.wait_ge(wo_lo_done, h + 1)
                    for b in range(B):
                        if b % HB == 0:
                            pe.wait_ge(out_drained, OUT_BANKS + m + b // HB + 1)
                        at = slice(b * L, (b + 1) * L)
                        bank = out_bank((2 * j + 2 + b) % OUT_BANKS, m + 2 + b + 1)
                        three(bank[:, :], [((attn_hi[:, at], attn_lo[:, at]), (wo_hi[:, j % 2, :], wo_lo[:, j % 2, :]))],
                              out_done)

            with pe.Fori(0, GROUPS - 1) as g:
                group(g, False)
            group(GROUPS - 1, True)

            end = OUT_FIRST + OUT_HEAD * H

            def ffn_transpose(b):
                n = ffn_chain(b, 0)
                pe.wait_ge(staged, B + b + 1)
                bank = out_bank(n % OUT_BANKS, end + n + 1)
                for c in range(C):
                    t = pe.transpose(bank[:, c * P:(c + 1) * P], stage(b)[:, c * P:(c + 1) * P], ident[:, :])
                t.then_inc(out_done, 1)

            def ffn_product(b):
                n = ffn_chain(b, 1)
                at = slice(b * L, (b + 1) * L)
                pe.wait_ge(out_drained, OUT_BANKS + end + ffn_chain(b, 0) + 1)
                bank = out_ps[n % OUT_BANKS]
                three(bank[:, :], [((xn_hi[:, c, at], xn_lo[:, c, at]), (wv_hi[:, c, :], wv_lo[:, c, :]))
                                   for c in range(C)], out_done)

            ffn_transpose(0)
            for b in range(B):
                if b + 1 < B:
                    ffn_transpose(b + 1)
                if b == 0:
                    pe.wait_ge(wv_lo_done, C * (GROUPS + 1))
                ffn_product(b)


def ffn_chain(b, product):
    if product:
        return 2 * b + 2 if b < B - 1 else 2 * b + 1
    return 2 * b - 1 if b else 0


def kernel(x, ctx_4096, mask_BxSxS2_bk0, L0_xattn_position_bias, L0_xattn_ln_weight, L0_xattn_w_q, L0_xattn_w_k,
           L0_xattn_w_v, L0_xattn_w_out, L0_ffn_w_codes, L0_ffn_absmax, L0_ffn_W_a, L0_ffn_W_b):
    import concourse.bacc as bacc
    from concourse.bass_utils import run_bass_kernel_spmd

    def head_weights(w):
        return np.asarray(w).reshape(H, DH, C, P).transpose(0, 3, 2, 1).reshape(H, P, C * DH)

    tokens_last = np.asarray(ctx_4096).reshape(2, HT, C, P).transpose(0, 3, 2, 1)
    wo = np.asarray(L0_xattn_w_out).reshape(D, H, DH).transpose(1, 2, 0)
    pos = np.asarray(L0_xattn_position_bias)
    wv = np.asarray(L0_xattn_w_v).reshape(GROUPS, G * DH, C, P).transpose(0, 3, 2, 1)
    codes = np.asarray(L0_ffn_w_codes).T.reshape(C, P, 2, SLICE).transpose(0, 2, 1, 3)
    absmax = np.asarray(L0_ffn_absmax).T.reshape(C, 2, 2, SLICE).transpose(0, 2, 1, 3)
    mask = np.ascontiguousarray(np.asarray(mask_BxSxS2_bk0).transpose(1, 0, 2)).reshape(L, B * L)
    data = {
        "x_dram": np.asarray(x),
        "ctx_dram": tokens_last,
        "mask_dram": mask.view(np.int32),
        "lnw_dram": np.asarray(L0_xattn_ln_weight).reshape(C, P).T,
        "qk_dram": np.concatenate([head_weights(L0_xattn_w_q), head_weights(L0_xattn_w_k)], axis=2),
        "ob_dram": np.concatenate([wo, pos], axis=2),
        "wv_dram": wv.reshape(GROUPS, P, C * G * DH),
        "codes_dram": codes.reshape(GROUPS, P, SLICE),
        "absmax_dram": absmax.reshape(GROUPS, 2, SLICE),
        "wa_dram": np.asarray(L0_ffn_W_a).T,
        "wb_dram": np.asarray(L0_ffn_W_b),
    }
    data = {name: np.ascontiguousarray(a) for name, a in data.items()}
    nc = bacc.Bacc("TRN2", target_bir_lowering=False, num_devices=1)
    ins = [nc.dram_tensor(name, a.shape, mybir.dt.from_np(a.dtype), kind="ExternalInput").ap()
           for name, a in data.items()]
    out = nc.dram_tensor("out_dram", (B, L, D), f32, kind="ExternalOutput").ap()
    xattn_ffn(nc, *ins, out)
    r = run_bass_kernel_spmd(nc, [data], core_ids=[0])
    return r.results[0]["out_dram"]
```

```python
from contextlib import ExitStack

import numpy as np
import concourse.bass as bass
from concourse import mybir

P = 128
B = 8
L = 128
D = 512
C = D // P
H = 32
DH = 128
G = 4
GROUPS = H // G
T = B * L
HT = T // 2
HB = B // 2
Q = 32
R = 16
LORA_SCALE = 32.0 / 16.0
EPS = 1e-5
MASKED = -3e38
QK = 2 * C * DH
OB = D + L
SLICE = C * D // GROUPS
NF4 = (-1.0, -0.6961928009986877, -0.5250730514526367, -0.39491748809814453, -0.28444138169288635,
       -0.18477343022823334, -0.09105003625154495, 0.0, 0.07958029955625534, 0.16093020141124725,
       0.24611230194568634, 0.33791524171829224, 0.44070982933044434, 0.5626170039176941,
       0.7229568362236023, 1.0)

PROJ_FIRST = B + C + 4
PROJ_GROUP = 4 * G + B
PROJ_END = PROJ_FIRST + PROJ_GROUP * (GROUPS - 1) + 4 * (G - 1)
PROJ_BANKS = 2
OUT_FIRST = 2 * C
OUT_HEAD = 2 + B
OUT_END = OUT_FIRST + OUT_HEAD * H
OUT_BANKS = 4

f32 = mybir.dt.float32
f32r = mybir.dt.float32r
bf16 = mybir.dt.bfloat16
i32 = mybir.dt.int32
u8 = mybir.dt.uint8
ALU = mybir.AluOpType
ACT = mybir.ActivationFunctionType
AX = mybir.AxisListType


def halves(h):
    return range(h * HB, (h + 1) * HB)


def xattn_ffn(nc, x_d, ctx_d, mask_d, lnw_d, qk_d, ob_d, wv_d, codes_d, absmax_d, wa_d, wb_d, out_d):
    with ExitStack() as ctx:
        def sb(name, shape, dt=f32):
            return ctx.enter_context(nc.sbuf_tensor(name, shape, dt))

        def sem(name):
            return ctx.enter_context(nc.semaphore(name))

        xn_hi = sb("xn_hi", [P, C, T], f32r)
        xn_lo = sb("xn_lo", [P, C, T], f32r)
        ctx_hi = sb("ctx_hi", [P, C, T], f32r)
        ctx_lo = sb("ctx_lo", [P, C, T], f32r)
        resid = sb("resid", [P, B, D])
        v = sb("v", [P, B, G * DH])
        qT = sb("qT", [P, T])
        kT = sb("kT", [P, T])
        qk_raw = sb("qk_raw", [P, 2, QK])
        qk_hi = sb("qk_hi", [P, 2, QK], f32r)
        qk_lo = sb("qk_lo", [P, 2, QK], f32r)
        ob_raw = sb("ob_raw", [P, 2, OB])
        wo_hi = sb("wo_hi", [P, 2, D], f32r)
        wo_lo = sb("wo_lo", [P, 2, D], f32r)
        wv_raw = sb("wv_raw", [P, C, G * DH])
        wv_hi = sb("wv_hi", [P, C, G * DH], f32r)
        wv_lo = sb("wv_lo", [P, C, G * DH], f32r)
        bias = sb("bias", [P, B, L])
        mask_add = sb("mask_add", [P, B, L], bf16)
        p = sb("p", [P, B, L])
        p_crossed = sb("p_crossed", [P, B, L])
        pT = sb("pT", [P, B, L])
        attn_hi = sb("attn_hi", [P, T], f32r)
        attn_lo = sb("attn_lo", [P, T], f32r)
        w_ffn = sb("w_ffn", [P, C * D])
        codes = sb("codes", [P, SLICE], i32)
        absmax = sb("absmax", [P, SLICE])
        scratch = sb("scratch", [P, 2 * SLICE])
        picked = scratch[:, 0:SLICE]
        level = scratch[:, SLICE:2 * SLICE]
        ident = sb("ident", [P, P])
        lnw = sb("lnw", [P, C])
        neg_max = sb("neg_max", [P, B])
        prob_sum = sb("prob_sum", [P, B])
        recip = sb("recip", [P, B])
        row_scale = sb("row_scale", [P, B])
        row_valid = sb("row_valid", [P, B])
        stats = sb("stats", [P, B, 6])
        mean_var = sb("mean_var", [P, B, 2])
        rstd = sb("rstd", [P, B])
        rms_a = sb("rms_a", [P, B])
        rms_b = sb("rms_b", [P, B])
        both = sb("both", [P, B])
        minus_half = sb("minus_half", [P, B])

        ctx_raw = v[:, :, :].rearrange("p b n -> p (b n)").rearrange("p (h c t) -> p h c t", h=2, c=C)
        mask_words = qk_raw[:, 1, 0:B * L // 4].bitcast(i32)
        mask_raw = mask_words.bitcast(u8).rearrange("p (b k) -> p b k", b=B)
        wa = p_crossed[0:R, 0:4, :].rearrange("p b k -> p (b k)")
        wb = p_crossed[0:R, 4:8, :].rearrange("p b k -> p (b k)")

        def tiles(t):
            flat = t.rearrange("p b k -> p (b k)")
            return [flat[:, i * D:(i + 1) * D] for i in range(2)]

        ffn_stage = tiles(p[:, :, :]) + tiles(pT[:, :, :])
        x_stage = ffn_stage + [qT[:, 0:D], qT[:, D:2 * D]] + tiles(p_crossed[:, :, :])

        def xT(b):
            return (qT, kT)[b % 4 // 2][:, b % 2 * D:(b % 2 + 1) * D]

        proj_ps = [ctx.enter_context(nc.psum_tensor(f"proj_ps{i}", [P, D], f32)) for i in range(PROJ_BANKS)]
        out_ps = [ctx.enter_context(nc.psum_tensor(f"out_ps{i}", [P, D], f32)) for i in range(OUT_BANKS)]
        s_ps = [ctx.enter_context(nc.psum_tensor(f"s_ps{i}", [P, HB, L], f32)) for i in range(2)]

        ctx_loaded = [sem(f"ctx_loaded{i}") for i in range(C)]
        ctx_rest_loaded = sem("ctx_rest_loaded")
        keys_loaded = sem("keys_loaded")
        x_loaded = [sem(f"x_loaded{i}") for i in range(2)]
        mask_loaded = sem("mask_loaded")
        small_loaded = sem("small_loaded")
        qk_loaded = [sem(f"qk_loaded{i}") for i in range(2)]
        ob_loaded = [sem(f"ob_loaded{i}") for i in range(2)]
        wv_loaded = sem("wv_loaded")
        codes_loaded = sem("codes_loaded")
        stored = sem("stored")

        keys_hi_done = sem("keys_hi_done")
        keys_lo_done = sem("keys_lo_done")
        ctx_hi_done = sem("ctx_hi_done")
        ctx_lo_done = sem("ctx_lo_done")
        qk_hi_done = sem("qk_hi_done")
        qk_lo_done = sem("qk_lo_done")
        wo_hi_done = sem("wo_hi_done")
        wo_lo_done = sem("wo_lo_done")
        wv_hi_done = sem("wv_hi_done")
        wv_lo_done = sem("wv_lo_done")
        mask_done = sem("mask_done")
        bias_done = sem("bias_done")
        const_done = sem("const_done")

        proj_done = sem("proj_done")
        proj_drained = sem("proj_drained")
        out_done = sem("out_done")
        out_drained = sem("out_drained")
        scores_done = sem("scores_done")
        biased = sem("biased")
        max_done = sem("max_done")
        exp_done = sem("exp_done")
        recip_done = sem("recip_done")
        row_scale_done = sem("row_scale_done")
        p_done = sem("p_done")
        crossed = sem("crossed")
        pT_done = sem("pT_done")
        attn_hi_done = sem("attn_hi_done")

        xT_hi_done = sem("xT_hi_done")
        xT_lo_done = sem("xT_lo_done")
        stats_done = sem("stats_done")
        norm_step = sem("norm_step")
        norm_done = sem("norm_done")
        staged = sem("staged")
        hidden_step = sem("hidden_step")
        ident_step = sem("ident_step")
        decode_step = sem("decode_step")
        decoded = sem("decoded")
        pool_passed = sem("pool_passed")

        block = ctx.enter_context(nc.Block())

        @block.sync
        def _(sp):
            def load_qk(h, slot):
                sp.dma_start(qk_raw[:, slot, :], qk_d[h]).then_inc(qk_loaded[slot], 16)

            def load_ob(h, slot):
                sp.dma_start(ob_raw[:, slot, :], ob_d[h]).then_inc(ob_loaded[slot], 16)

            def load_wv(g):
                sp.dma_start(wv_raw[:, :, :].rearrange("p c n -> p (c n)"), wv_d[g]).then_inc(wv_loaded, 16)

            def load_codes(g):
                sp.dma_start(codes[:, :], codes_d[g]).then_inc(codes_loaded, 16)
                for s in range(2):
                    sp.dma_start(absmax[64 * s:64 * s + 64, :],
                                 absmax_d[g, s].partition_broadcast(64)).then_inc(codes_loaded, 16)

            keys = slice(C * DH, QK)
            sp.dma_start(qk_raw[:, 0, keys], qk_d[0, :, keys]).then_inc(keys_loaded, 16)
            for c in range(C):
                sp.dma_start(ctx_raw[:, 0, c, :], ctx_d[0, :, c]).then_inc(ctx_loaded[c], 16)
            sp.dma_start(lnw[:, :], lnw_d).then_inc(small_loaded, 16)
            sp.dma_start(wa, wa_d).then_inc(small_loaded, 16)
            sp.dma_start(wb, wb_d).then_inc(small_loaded, 16)
            load_wv(0)
            sp.dma_start(ctx_raw[:, 1, :, :], ctx_d[1]).then_inc(ctx_rest_loaded, 16)
            for hf in range(2):
                sp.dma_start(resid[:, hf * HB:(hf + 1) * HB, :],
                             x_d[hf * HB:(hf + 1) * HB].rearrange("b t d -> t b d")).then_inc(x_loaded[hf], 16)
            sp.dma_start(qk_raw[:, 0, 0:C * DH], qk_d[0, :, 0:C * DH]).then_inc(qk_loaded[0], 16)
            sp.dma_start(mask_words, mask_d).then_inc(mask_loaded, 16)
            load_ob(0, 0)
            load_ob(1, 1)
            load_codes(0)
            sp.wait_ge(mask_done, 2)
            load_qk(1, 1)
            for h in range(2):
                sp.wait_ge(qk_lo_done, h + 1)
                load_qk(h + 2, h)
            sp.wait_ge(wo_lo_done, 1)
            sp.wait_ge(bias_done, 1)
            load_ob(2, 0)

            def group(g, last):
                if not last:
                    sp.wait_ge(wv_lo_done, C * (g + 1))
                    load_wv(g + 1)
                for j in range(G):
                    h = G * g + j
                    if not (last and j + 4 >= G):
                        sp.wait_ge(qk_lo_done, h + 3)
                        load_qk(h + 4, j % 2)
                    if not (last and j + 3 >= G):
                        sp.wait_ge(wo_lo_done, h + 2)
                        sp.wait_ge(bias_done, h + 2)
                        load_ob(h + 3, (j + 1) % 2)
                if not last:
                    sp.wait_ge(decoded, g + 1)
                    load_codes(g + 1)

            with sp.Fori(0, GROUPS - 1) as g:
                group(g, False)
            group(GROUPS - 1, True)

            for b in range(B):
                sp.wait_ge(out_drained, OUT_BANKS + OUT_END + b + 1)
                sp.dma_start(out_d[b], resid[:, b, :]).then_inc(stored, 16)
            sp.wait_ge(stored, 16 * B)

        @block.gpsimd
        def _(pool):
            def passed(s, value):
                pool.wait_ge(s, value)
                pool.sem_inc(pool_passed, 1)

            pool.memset(minus_half[:, :], -0.5).then_inc(const_done, 1)
            pool.memset(ident[:, :], 0.0).then_inc(ident_step, 1)
            pool.wait_ge(ident_step, 1)
            pool.affine_select(out=ident[:, :], in_=ident[:, :], compare_op=ALU.not_equal, fill=1.0, base=0,
                               pattern=[[-1, P]], channel_multiplier=1).then_inc(const_done, 1)

            for c in range(C):
                pool.wait_ge(wv_hi_done, c + 1)
                pool.tensor_tensor(wv_lo[:, c, :], wv_raw[:, c, :], wv_hi[:, c, :].bitcast(f32),
                                   ALU.subtract).then_inc(wv_lo_done, 1)

            steps = [0]

            def norm(ins):
                ins.then_inc(norm_step, 1)
                steps[0] += 1
                pool.wait_ge(norm_step, steps[0])

            pool.wait_ge(const_done, 2)
            for hf in range(2):
                bs = slice(hf * HB, (hf + 1) * HB)
                var = mean_var[:, bs, 1]
                pool.wait_ge(stats_done, 2 * HB * (hf + 1))
                norm(pool.tensor_scalar(rms_a[:, bs], var, EPS, None, ALU.add))
                norm(pool.tensor_tensor(rstd[:, bs], rms_a[:, bs], minus_half[:, bs], ALU.pow))
                norm(pool.tensor_tensor(rms_a[:, bs], rstd[:, bs], rstd[:, bs], ALU.mult))
                norm(pool.tensor_tensor(rms_b[:, bs], rms_a[:, bs], var, ALU.mult))
                norm(pool.tensor_scalar(rms_a[:, bs], rms_b[:, bs], EPS, None, ALU.add))
                norm(pool.tensor_tensor(rms_b[:, bs], rms_a[:, bs], minus_half[:, bs], ALU.pow))
                pool.tensor_tensor(both[:, bs], rms_b[:, bs], rstd[:, bs], ALU.mult).then_inc(norm_done, 1)

            def make_bias(slot):
                pos = ob_raw[:, slot, D:OB].rearrange("p (o k) -> p o k", o=1).broadcast_to([P, B, L])
                pool.tensor_tensor(bias[:, :, :], pos, mask_add[:, :, :], ALU.add).then_inc(bias_done, 1)

            for b in range(B):
                if b == HB:
                    pool.wait_ge(mask_done, 2)
                    pool.wait_ge(ob_loaded[0], 16)
                    make_bias(0)
                pool.wait_ge(staged, b + 1)
                pool.tensor_scalar(scratch[:, :], resid[:, b, :], mean_var[:, b, 0:1], rstd[:, b:b + 1],
                                   ALU.subtract, ALU.mult).then_inc(hidden_step, 1)
                pool.wait_ge(hidden_step, 2 * b + 1)
                pool.tensor_tensor(resid[:, b, :], resid[:, b, :], scratch[:, :], ALU.add).then_inc(hidden_step, 1)
                pool.wait_ge(hidden_step, 2 * b + 2)

            per_slice = 2 * (len(NF4) - 1) + 1

            def decode(g, quarter):
                step = [per_slice * g + (0, 7, 13, 21)[quarter]]

                def then(ins):
                    ins.then_inc(decode_step, 1)
                    step[0] += 1
                    passed(decode_step, step[0])

                if quarter == 0:
                    passed(codes_loaded, 48 * (g + 1))
                for code in range(4 * quarter, 4 * quarter + 4):
                    value = NF4[code]
                    if value == 0.0:
                        continue
                    match = ALU.is_ge if code == len(NF4) - 1 else ALU.is_equal
                    then(pool.tensor_scalar(level if code == 0 else picked, codes[:, :], float(code), value,
                                            match, ALU.mult))
                    if code:
                        then(pool.tensor_tensor(level, level, picked, ALU.add))
                if quarter == 3:
                    then(pool.tensor_tensor(picked, level, absmax[:, :], ALU.mult))
                    at = bass.ds(g * SLICE, SLICE)
                    then(pool.tensor_tensor(w_ffn[:, at], w_ffn[:, at], picked, ALU.add))
                    pool.sem_inc(decoded, 1)

            def group(g, last):
                for j in range(G):
                    h = G * g + j
                    if not (last and j == G - 1):
                        passed(p_done, 2 * h + 2)
                        passed(ob_loaded[(j + 1) % 2], 16 * (2 * g + (j + 1) // 2 + 1))
                        make_bias((j + 1) % 2)
                    for quarter in (((0, 1), (2, 3), (), ())[j] if last else (j,)):
                        decode(g, quarter)

            with pool.Fori(0, GROUPS - 1) as g:
                group(g, False)
            group(GROUPS - 1, True)

            def xT_low(b):
                pool.wait_ge(xT_hi_done, b + 1)
                pool.wait_ge(proj_drained, PROJ_END + b + 1)
                at = slice(b * L, (b + 1) * L)
                pool.tensor_tensor(xn_lo[:, :, at], xT(b).rearrange("p (c t) -> p c t", c=C),
                                   xn_hi[:, :, at].bitcast(f32), ALU.subtract).then_inc(xT_lo_done, 1)

            lag = 4
            for b in range(B + lag):
                if b < B:
                    one = slice(b, b + 1)
                    pool.wait_ge(stats_done, 2 * B + 2 * (b + 1))
                    norm(pool.tensor_scalar(rms_a[:, one], mean_var[:, b, 1:2], EPS, None, ALU.add))
                    pool.tensor_tensor(rstd[:, one], rms_a[:, one], minus_half[:, one],
                                       ALU.pow).then_inc(norm_done, 1)
                if b >= lag:
                    xT_low(b - lag)

        @block.scalar
        def _(act):
            def copy(out, in_, **kw):
                return act.activation(out, in_, ACT.Copy, **kw)

            def split_wv(c, source):
                copy(wv_hi[:, c, :], source).then_inc(wv_hi_done, 1)

            def drain(n, bank, out, **kw):
                act.wait_ge(proj_done, n + 1)
                copy(out, proj_ps[bank][:, :], **kw).then_inc(proj_drained, 1)

            keys = slice(C * DH, QK)
            act.wait_ge(keys_loaded, 16)
            copy(qk_hi[:, 0, keys], qk_raw[:, 0, keys]).then_inc(keys_hi_done, 1)
            for c in range(C):
                act.wait_ge(ctx_loaded[c], 16)
                copy(ctx_hi[:, c, 0:HT], ctx_raw[:, 0, c, :]).then_inc(ctx_hi_done, 1)
            act.wait_ge(wv_loaded, 16)
            for c in range(C):
                split_wv(c, wv_raw[:, c, :])
            drain(0, 0, kT[:, 0:HT])
            for c in range(C):
                drain(1 + c, (1 + c) % 2, w_ffn[:, c * D:(c + 1) * D], scale=LORA_SCALE)
            act.wait_ge(ctx_rest_loaded, 16)
            for c in range(C):
                copy(ctx_hi[:, c, HT:T], ctx_raw[:, 1, c, :]).then_inc(ctx_hi_done, 1)
            for b in range(HB):
                drain(1 + C + b, (1 + b) % 2, v[:, b, :])
            act.wait_ge(qk_loaded[0], 16)
            copy(qk_hi[:, 0, 0:C * DH], qk_raw[:, 0, 0:C * DH]).then_inc(qk_hi_done, 1)
            drain(1 + C + HB, 1, kT[:, HT:T])

            def xn_high(hf):
                for c in range(C):
                    act.wait_ge(out_done, C * hf + c + 1)
                    copy(xn_hi[:, c, hf * HT:(hf + 1) * HT], out_ps[c][:, :],
                         scale=lnw[:, c:c + 1]).then_inc(attn_hi_done, 1)

            act.wait_ge(small_loaded, 48)
            for b in range(HB, B):
                drain(2 + C + b, b % 2, v[:, b, :])
                if b == B - 2:
                    xn_high(0)
            xn_high(1)
            act.wait_ge(qk_loaded[1], 16)
            copy(qk_hi[:, 1, :], qk_raw[:, 1, :]).then_inc(qk_hi_done, 1)
            for hf in range(2):
                drain(B + C + 2 + hf, hf, qT[:, hf * HT:(hf + 1) * HT])
            act.wait_ge(ob_loaded[0], 16)
            copy(wo_hi[:, 0, :], ob_raw[:, 0, 0:D]).then_inc(wo_hi_done, 1)
            act.wait_ge(qk_loaded[0], 32)
            copy(qk_hi[:, 0, :], qk_raw[:, 0, :]).then_inc(qk_hi_done, 1)

            def exps(h):
                for hf in range(2):
                    act.wait_ge(max_done, 2 * h + hf + 1)
                    for b in halves(hf):
                        e = act.activation(p[:, b, :], p[:, b, :], ACT.Exp, bias=neg_max[:, b:b + 1],
                                           accum_out=prob_sum[:, b:b + 1])
                    e.then_inc(exp_done, 1)

            def group(g, last):
                for j in range(G):
                    h = G * g + j
                    final = last and j == G - 1
                    n = PROJ_FIRST + PROJ_GROUP * g + 4 * j
                    if not final:
                        for hf in range(2):
                            drain(n + hf, hf, qT[:, hf * HT:(hf + 1) * HT])
                        slot = (j + 1) % 2
                        act.wait_ge(ob_loaded[slot], 16 * (2 * g + (j + 1) // 2 + 1))
                        act.wait_ge(out_done, OUT_FIRST + OUT_HEAD * h)
                        copy(wo_hi[:, slot, :], ob_raw[:, slot, 0:D]).then_inc(wo_hi_done, 1)
                        for hf in range(2):
                            drain(n + 2 + hf, hf, kT[:, hf * HT:(hf + 1) * HT])
                    for hf in range(2):
                        act.wait_ge(out_done, OUT_FIRST + OUT_HEAD * h + hf + 1)
                        copy(attn_hi[:, hf * HT:(hf + 1) * HT],
                             out_ps[(2 * j + hf) % OUT_BANKS][:, :]).then_inc(attn_hi_done, 1)
                    if not (last and j + 3 >= G):
                        slot = (j + 1) % 2
                        act.wait_ge(qk_loaded[slot], 16 * (2 * g + (j + 3) // 2 + 1))
                        copy(qk_hi[:, slot, :], qk_raw[:, slot, :]).then_inc(qk_hi_done, 1)
                    if not last:
                        if j == 0:
                            act.wait_ge(wv_loaded, 16 * (g + 2))
                        for c in ((0, 1), (2,), (3,), ())[j]:
                            split_wv(c, wv_raw[:, c, :])
                    else:
                        act.wait_ge(decoded, GROUPS if j == G - 1 else GROUPS - 1)
                        split_wv(j, w_ffn[:, j * D:(j + 1) * D])
                    if not final:
                        exps(h + 1)
                    if not last and j == G - 1:
                        for b in range(B):
                            drain(n + 4 + b, b % 2, v[:, b, :])

            exps(0)
            with act.Fori(0, GROUPS - 1) as g:
                group(g, False)
            group(GROUPS - 1, True)

            for b in range(B):
                act.wait_ge(proj_done, PROJ_END + b + 1)
                bank = proj_ps[b % 2][:, :]
                copy(xn_hi[:, :, b * L:(b + 1) * L], bank.rearrange("p (c t) -> p c t", c=C)).then_inc(xT_hi_done, 1)
                if b >= 4:
                    act.wait_ge(xT_lo_done, b - 3)
                copy(xT(b), bank).then_inc(proj_drained, 1)

        @block.vector
        def _(dve):
            def lo(out, whole, hi):
                return dve.tensor_tensor(out, whole, hi.bitcast(f32), ALU.subtract)

            def out_count(h):
                return OUT_FIRST + OUT_HEAD * h

            dve.memset(neg_max[:, :], 0.0).then_inc(out_drained, OUT_BANKS)

            def tile_stats(b, before):
                dve.bn_stats(stats[:, b, :], resid[:, b, :]).then_inc(stats_done, 1)
                dve.wait_ge(stats_done, before + 1)
                dve.bn_aggr(mean_var[:, b, :], stats[:, b, :]).then_inc(stats_done, 1)

            keys = slice(C * DH, QK)
            dve.wait_ge(keys_hi_done, 1)
            lo(qk_lo[:, 0, keys], qk_raw[:, 0, keys], qk_hi[:, 0, keys]).then_inc(keys_lo_done, 1)
            for c in range(C):
                dve.wait_ge(ctx_hi_done, c + 1)
                lo(ctx_lo[:, c, 0:HT], ctx_raw[:, 0, c, :], ctx_hi[:, c, 0:HT]).then_inc(ctx_lo_done, 1)
            for c in range(C):
                dve.wait_ge(ctx_hi_done, C + c + 1)
                lo(ctx_lo[:, c, HT:T], ctx_raw[:, 1, c, :], ctx_hi[:, c, HT:T]).then_inc(ctx_lo_done, 1)
            for hf in range(2):
                dve.wait_ge(x_loaded[hf], 16)
                for b in halves(hf):
                    tile_stats(b, 2 * b)
            dve.wait_ge(proj_done, 1 + C)
            for hf in range(2):
                dve.wait_ge(norm_done, hf + 1)
                for b in halves(hf):
                    dve.tensor_scalar(x_stage[b], resid[:, b, :], mean_var[:, b, 0:1], both[:, b:b + 1],
                                      ALU.subtract, ALU.mult).then_inc(staged, 1)
            dve.wait_ge(qk_hi_done, 1)
            lo(qk_lo[:, 0, 0:C * DH], qk_raw[:, 0, 0:C * DH], qk_hi[:, 0, 0:C * DH]).then_inc(qk_lo_done, 1)
            dve.wait_ge(mask_loaded, 16)
            dve.tensor_scalar(mask_add[:, :, :], mask_raw, 1.0, -MASKED, ALU.subtract, ALU.mult).then_inc(mask_done, 1)
            dve.tensor_reduce(row_valid[:, :], mask_raw, AX.X, ALU.max).then_inc(mask_done, 1)

            for hf in range(2):
                for c in range(C):
                    dve.wait_ge(attn_hi_done, C * hf + c + 1)
                    dve.scalar_tensor_tensor(
                        xn_lo[:, c, hf * HT:(hf + 1) * HT], out_ps[c][:, :], lnw[:, c:c + 1],
                        xn_hi[:, c, hf * HT:(hf + 1) * HT].bitcast(f32), ALU.mult, ALU.subtract,
                    ).then_inc(out_drained, 1)
            dve.wait_ge(qk_hi_done, 2)
            lo(qk_lo[:, 1, :], qk_raw[:, 1, :], qk_hi[:, 1, :]).then_inc(qk_lo_done, 1)
            dve.wait_ge(wo_hi_done, 1)
            lo(wo_lo[:, 0, :], ob_raw[:, 0, 0:D], wo_hi[:, 0, :]).then_inc(wo_lo_done, 1)

            def bias_and_max(h):
                for hf in range(2):
                    bs = slice(hf * HB, (hf + 1) * HB)
                    dve.wait_ge(scores_done, 2 * h + hf + 1)
                    if hf == 0:
                        dve.wait_ge(bias_done, h + 1)
                    dve.tensor_tensor(p[:, bs, :], s_ps[hf][:, :, :], bias[:, bs, :],
                                      ALU.add).then_inc(biased, 1)
                    dve.wait_ge(biased, 2 * h + hf + 1)
                    dve.tensor_reduce(neg_max[:, bs], p[:, bs, :], AX.X, ALU.max,
                                      negate=True).then_inc(max_done, 1)

            def group(g, last):
                for j in range(G):
                    h = G * g + j
                    final = last and j == G - 1
                    for hf in range(2):
                        bs = slice(hf * HB, (hf + 1) * HB)
                        dve.wait_ge(exp_done, 2 * h + hf + 1)
                        dve.reciprocal(recip[:, bs], prob_sum[:, bs]).then_inc(recip_done, 1)
                        dve.wait_ge(recip_done, 2 * h + hf + 1)
                        dve.tensor_tensor(row_scale[:, bs], recip[:, bs], row_valid[:, bs],
                                          ALU.mult).then_inc(row_scale_done, 1)
                        dve.wait_ge(row_scale_done, 2 * h + hf + 1)
                        scale = row_scale[:, bs].rearrange("p (b o) -> p b o", o=1).broadcast_to([P, HB, L])
                        dve.tensor_tensor(p[:, bs, :], p[:, bs, :], scale, ALU.mult).then_inc(p_done, 1)
                    dve.wait_ge(p_done, 2 * h + 2)
                    for i in range(P // Q):
                        for k in range(P // Q):
                            a, b = slice(Q * i, Q * (i + 1)), slice(Q * k, Q * (k + 1))
                            e = dve.tensor_copy(p_crossed[b, :, a], p[a, :, b])
                    e.then_inc(crossed, 1)
                    dve.wait_ge(crossed, h + 1)
                    for hf in range(2):
                        bs = slice(hf * HB, (hf + 1) * HB)
                        dve.transpose(pT[:, bs, :].rearrange("p b q -> p (b q)"),
                                      p_crossed[:, bs, :].rearrange("p b q -> p (b q)")).then_inc(pT_done, 1)
                    if not (last and j + 2 >= G):
                        slot = j % 2
                        dve.wait_ge(qk_hi_done, h + 3)
                        lo(qk_lo[:, slot, :], qk_raw[:, slot, :], qk_hi[:, slot, :]).then_inc(qk_lo_done, 1)
                    if not final:
                        slot = (j + 1) % 2
                        dve.wait_ge(wo_hi_done, h + 2)
                        lo(wo_lo[:, slot, :], ob_raw[:, slot, 0:D], wo_hi[:, slot, :]).then_inc(wo_lo_done, 1)
                    for hf in range(2):
                        dve.wait_ge(attn_hi_done, 2 * C + 2 * h + hf + 1)
                        at = slice(hf * HT, (hf + 1) * HT)
                        lo(attn_lo[:, at], out_ps[(2 * j + hf) % OUT_BANKS][:, :],
                           attn_hi[:, at]).then_inc(out_drained, 1)
                    if last:
                        dve.wait_ge(wv_hi_done, C * GROUPS + j + 1)
                        lo(wv_lo[:, j, :], w_ffn[:, j * D:(j + 1) * D], wv_hi[:, j, :]).then_inc(wv_lo_done, 1)
                    for b in range(B):
                        dve.wait_ge(out_done, out_count(h) + 2 + b + 1)
                        if b == 0:
                            dve.wait_ge(hidden_step, 2 * B)
                            dve.wait_ge(out_drained, OUT_BANKS + out_count(h) + 2)
                        dve.tensor_tensor(resid[:, b, :], out_ps[(2 * j + 2 + b) % OUT_BANKS][:, :],
                                          resid[:, b, :], ALU.add).then_inc(out_drained, 1)
                        if b == HB - 1 and not final:
                            bias_and_max(h + 1)
                        if final:
                            dve.wait_ge(out_drained, OUT_BANKS + out_count(h) + 2 + b + 1)
                            tile_stats(b, 2 * B + 2 * b)
                            if b >= 1:
                                ffn_norm(b - 1)
                    if not last:
                        for c in ((0, 1), (2,), (3,), ())[j]:
                            dve.wait_ge(wv_hi_done, C * (g + 1) + c + 1)
                            lo(wv_lo[:, c, :], wv_raw[:, c, :], wv_hi[:, c, :]).then_inc(wv_lo_done, 1)

            def ffn_norm(b):
                dve.wait_ge(norm_done, 2 + b + 1)
                if b >= 4:
                    dve.wait_ge(proj_done, PROJ_END + b - 4 + 1)
                dve.tensor_scalar(ffn_stage[b % 4], resid[:, b, :], mean_var[:, b, 0:1], rstd[:, b:b + 1],
                                  ALU.subtract, ALU.mult).then_inc(staged, 1)

            bias_and_max(0)
            with dve.Fori(0, GROUPS - 1) as g:
                group(g, False)
            group(GROUPS - 1, True)
            ffn_norm(B - 1)

            for b in range(B):
                dve.wait_ge(out_done, OUT_END + b + 1)
                dve.tensor_tensor(resid[:, b, :], out_ps[b % OUT_BANKS][:, :], resid[:, b, :],
                                  ALU.add).then_inc(out_drained, 1)

        @block.tensor
        def _(pe):
            def three(out, pairs, sem_done):
                n = 3 * len(pairs)
                i = 0
                for (l_hi, l_lo), (r_hi, r_lo) in pairs:
                    for l, r in ((l_hi, r_hi), (l_hi, r_lo), (l_lo, r_hi)):
                        m = pe.matmul(out, l, r, start=(i == 0), stop=(i == n - 1))
                        i += 1
                m.then_inc(sem_done, 1)

            def proj_bank(n, bank, first=False):
                if not first:
                    pe.wait_ge(proj_drained, n - PROJ_BANKS + 1)
                return proj_ps[bank][:, :]

            def values(n, bank, b, first=False):
                at = slice(b * L, (b + 1) * L)
                three(proj_bank(n, bank, first),
                      [((ctx_hi[:, c, at], ctx_lo[:, c, at]), (wv_hi[:, c, :], wv_lo[:, c, :])) for c in range(C)],
                      proj_done)

            def project(n, slot, which, hf):
                a_hi, a_lo = ((xn_hi, xn_lo), (ctx_hi, ctx_lo))[which]
                at = slice(hf * HT, (hf + 1) * HT)

                def w(t, c):
                    k = (which * C + c) * DH
                    return t[:, slot, k:k + DH]

                three(proj_bank(n, hf),
                      [((w(qk_hi, c), w(qk_lo, c)), (a_hi[:, c, at], a_lo[:, c, at])) for c in range(C)],
                      proj_done)

            def first_keys():
                i = 0
                for c in range(C):
                    pe.wait_ge(ctx_lo_done, c + 1)
                    k = (C + c) * DH
                    w_hi, w_lo = (t[:, 0, k:k + DH] for t in (qk_hi, qk_lo))
                    for l, r in ((w_hi, ctx_hi), (w_hi, ctx_lo), (w_lo, ctx_hi)):
                        m = pe.matmul(proj_ps[0][:, :], l, r[:, c, 0:HT], start=(i == 0), stop=(i == 3 * C - 1))
                        i += 1
                m.then_inc(proj_done, 1)

            def scores(h, n, first=False):
                pe.wait_ge(proj_drained, n)
                if not first:
                    pe.wait_ge(biased, 2 * h)
                for hf in range(2):
                    for i, b in enumerate(halves(hf)):
                        at = slice(b * L, (b + 1) * L)
                        s = pe.matmul(s_ps[hf][:, i, :], qT[:, at], kT[:, at], start=True, stop=True)
                    s.then_inc(scores_done, 1)

            def out_bank(n_bank, count):
                pe.wait_ge(out_drained, count)
                return out_ps[n_bank]

            pe.wait_ge(keys_lo_done, 1)
            first_keys()
            pe.wait_ge(small_loaded, 48)
            for c in range(C):
                bank = proj_ps[1][:, :] if c == 0 else proj_bank(1 + c, (1 + c) % 2)
                pe.matmul(bank, wa[:, c * P:(c + 1) * P], wb, start=True, stop=True).then_inc(proj_done, 1)
            pe.wait_ge(wv_lo_done, C)
            for b in range(HB):
                values(1 + C + b, (1 + b) % 2, b)
            pe.wait_ge(ctx_lo_done, 2 * C)
            project(1 + C + HB, 0, 1, 1)

            def transpose_x(hf):
                pe.wait_ge(staged, HB * (hf + 1))
                for c in range(C):
                    bank = out_bank(c, C * hf + c + 1)
                    for i, b in enumerate(halves(hf)):
                        t = pe.transpose(bank[:, i * P:(i + 1) * P], x_stage[b][:, c * P:(c + 1) * P], ident[:, :])
                    t.then_inc(out_done, 1)

            pe.wait_ge(const_done, 2)
            for b in range(HB, B):
                values(2 + C + b, b % 2, b)
                if b == B - 2:
                    transpose_x(0)
            transpose_x(1)
            pe.wait_ge(qk_lo_done, 1)
            for hf in range(2):
                pe.wait_ge(out_drained, OUT_BANKS + C * (hf + 1))
                project(B + C + 2 + hf, 0, 0, hf)

            def group(g, last):
                for j in range(G):
                    h = G * g + j
                    final = last and j == G - 1
                    n = PROJ_FIRST + PROJ_GROUP * g + 4 * j
                    m = OUT_FIRST + OUT_HEAD * h
                    if not final:
                        slot = (j + 1) % 2
                        pe.wait_ge(qk_lo_done, h + 2)
                        for k in range(4):
                            project(n + k, slot, k // 2, k % 2)
                    for hf in range(2):
                        pe.wait_ge(pT_done, 2 * h + hf + 1)
                        bank = out_bank((2 * j + hf) % OUT_BANKS, m + hf + 1)
                        for i, b in enumerate(halves(hf)):
                            o = pe.matmul(bank[:, i * L:(i + 1) * L], v[:, b, j * DH:(j + 1) * DH], pT[:, b, :],
                                          start=True, stop=True)
                        o.then_inc(out_done, 1)
                    if not final:
                        scores(h + 1, n + 4)
                    pe.wait_ge(wo_lo_done, h + 1)
                    for b in range(B):
                        if b % HB == 0:
                            pe.wait_ge(out_drained, OUT_BANKS + m + b // HB + 1)
                        at = slice(b * L, (b + 1) * L)
                        bank = out_bank((2 * j + 2 + b) % OUT_BANKS, m + 2 + b + 1)
                        three(bank[:, :], [((attn_hi[:, at], attn_lo[:, at]), (wo_hi[:, j % 2, :], wo_lo[:, j % 2, :]))],
                              out_done)
                    if not last and j == G - 1:
                        pe.wait_ge(wv_lo_done, C * (g + 2))
                        for b in range(B):
                            values(n + 4 + b, b % 2, b)

            scores(0, PROJ_FIRST, first=True)
            with pe.Fori(0, GROUPS - 1) as g:
                group(g, False)
            group(GROUPS - 1, True)

            def ffn_transpose(b):
                pe.wait_ge(staged, B + b + 1)
                bank = proj_bank(PROJ_END + b, b % 2)
                for c in range(C):
                    t = pe.transpose(bank[:, c * P:(c + 1) * P], ffn_stage[b % 4][:, c * P:(c + 1) * P], ident[:, :])
                t.then_inc(proj_done, 1)

            def ffn_product(b):
                at = slice(b * L, (b + 1) * L)
                pe.wait_ge(xT_lo_done, b + 1)
                bank = out_bank(b % OUT_BANKS, OUT_END + b + 1)
                three(bank[:, :], [((xn_hi[:, c, at], xn_lo[:, c, at]), (wv_hi[:, c, :], wv_lo[:, c, :]))
                                   for c in range(C)], out_done)

            ffn_transpose(0)
            for b in range(B):
                if b + 1 < B:
                    ffn_transpose(b + 1)
                if b == 0:
                    pe.wait_ge(wv_lo_done, C * (GROUPS + 1))
                ffn_product(b)


def kernel(x, ctx_4096, mask_BxSxS2_bk0, L0_xattn_position_bias, L0_xattn_ln_weight, L0_xattn_w_q, L0_xattn_w_k,
           L0_xattn_w_v, L0_xattn_w_out, L0_ffn_w_codes, L0_ffn_absmax, L0_ffn_W_a, L0_ffn_W_b):
    import concourse.bacc as bacc
    from concourse.bass_utils import run_bass_kernel_spmd

    def head_weights(w):
        return np.asarray(w).reshape(H, DH, C, P).transpose(0, 3, 2, 1).reshape(H, P, C * DH)

    tokens_last = np.asarray(ctx_4096).reshape(2, HT, C, P).transpose(0, 3, 2, 1)
    wo = np.asarray(L0_xattn_w_out).reshape(D, H, DH).transpose(1, 2, 0)
    pos = np.asarray(L0_xattn_position_bias)
    wv = np.asarray(L0_xattn_w_v).reshape(GROUPS, G * DH, C, P).transpose(0, 3, 2, 1)
    codes = np.asarray(L0_ffn_w_codes).T.reshape(C, P, 2, SLICE).transpose(0, 2, 1, 3)
    absmax = np.asarray(L0_ffn_absmax).T.reshape(C, 2, 2, SLICE).transpose(0, 2, 1, 3)
    mask = np.ascontiguousarray(np.asarray(mask_BxSxS2_bk0).transpose(1, 0, 2)).reshape(L, B * L)
    data = {
        "x_dram": np.asarray(x),
        "ctx_dram": tokens_last,
        "mask_dram": mask.view(np.int32),
        "lnw_dram": np.asarray(L0_xattn_ln_weight).reshape(C, P).T,
        "qk_dram": np.concatenate([head_weights(L0_xattn_w_q), head_weights(L0_xattn_w_k)], axis=2),
        "ob_dram": np.concatenate([wo, pos], axis=2),
        "wv_dram": wv.reshape(GROUPS, P, C * G * DH),
        "codes_dram": codes.reshape(GROUPS, P, SLICE),
        "absmax_dram": absmax.reshape(GROUPS, 2, SLICE),
        "wa_dram": np.asarray(L0_ffn_W_a).T,
        "wb_dram": np.asarray(L0_ffn_W_b),
    }
    data = {name: np.ascontiguousarray(a) for name, a in data.items()}
    nc = bacc.Bacc("TRN2", target_bir_lowering=False, num_devices=1)
    ins = [nc.dram_tensor(name, a.shape, mybir.dt.from_np(a.dtype), kind="ExternalInput").ap()
           for name, a in data.items()]
    out = nc.dram_tensor("out_dram", (B, L, D), f32, kind="ExternalOutput").ap()
    xattn_ffn(nc, *ins, out)
    r = run_bass_kernel_spmd(nc, [data], core_ids=[0])
    return r.results[0]["out_dram"]
```

```python
from contextlib import ExitStack

import numpy as np
import concourse.bass as bass
from concourse import mybir

P = 128
B = 8
L = 128
D = 512
C = D // P
H = 32
DH = 128
G = 4
GROUPS = H // G
T = B * L
HT = T // 2
HB = B // 2
Q = 32
R = 16
LORA_SCALE = 32.0 / 16.0
EPS = 1e-5
MASKED = -3e38
QK = 2 * C * DH
OB = D + L
SLICE = C * D // GROUPS
NF4 = (-1.0, -0.6961928009986877, -0.5250730514526367, -0.39491748809814453, -0.28444138169288635,
       -0.18477343022823334, -0.09105003625154495, 0.0, 0.07958029955625534, 0.16093020141124725,
       0.24611230194568634, 0.33791524171829224, 0.44070982933044434, 0.5626170039176941,
       0.7229568362236023, 1.0)

PROJ_FIRST = B + C + 4
PROJ_GROUP = 4 * G + B
PROJ_END = PROJ_FIRST + PROJ_GROUP * (GROUPS - 1) + 4 * (G - 1)
PROJ_BANKS = 2
OUT_FIRST = 2 * C
OUT_HEAD = 2 + B
OUT_END = OUT_FIRST + OUT_HEAD * H
OUT_BANKS = 4
NORMALISE_AFTER = (0, 2)
TURN_BEFORE = (5, 7)
FFN_TRANSPOSE_BEFORE = 6
WARM_UP = 10

f32 = mybir.dt.float32
f32r = mybir.dt.float32r
bf16 = mybir.dt.bfloat16
i32 = mybir.dt.int32
u8 = mybir.dt.uint8
ALU = mybir.AluOpType
ACT = mybir.ActivationFunctionType
AX = mybir.AxisListType


def halves(h):
    return range(h * HB, (h + 1) * HB)


def xattn_ffn(nc, x_d, ctx_d, mask_d, lnw_d, qk_d, ob_d, wv_d, codes_d, absmax_d, wa_d, wb_d, out_d):
    with ExitStack() as ctx:
        def sb(name, shape, dt=f32):
            return ctx.enter_context(nc.sbuf_tensor(name, shape, dt))

        def sem(name):
            return ctx.enter_context(nc.semaphore(name))

        xn_hi = sb("xn_hi", [P, C, T], f32r)
        xn_lo = sb("xn_lo", [P, C, T], f32r)
        ctx_hi = sb("ctx_hi", [P, C, T], f32r)
        ctx_lo = sb("ctx_lo", [P, C, T], f32r)
        resid = sb("resid", [P, B, D])
        v = sb("v", [P, B, G * DH])
        qT = sb("qT", [P, T])
        kT = sb("kT", [P, T])
        qk_raw = sb("qk_raw", [P, 2, QK])
        qk_hi = sb("qk_hi", [P, 2, QK], f32r)
        qk_lo = sb("qk_lo", [P, 2, QK], f32r)
        ob_raw = sb("ob_raw", [P, 2, OB])
        wo_hi = sb("wo_hi", [P, 2, D], f32r)
        wo_lo = sb("wo_lo", [P, 2, D], f32r)
        wv_raw = sb("wv_raw", [P, C, G * DH])
        wv_hi = sb("wv_hi", [P, C, G * DH], f32r)
        wv_lo = sb("wv_lo", [P, C, G * DH], f32r)
        bias = sb("bias", [P, B, L])
        mask_add = sb("mask_add", [P, B, L], bf16)
        p = sb("p", [P, B, L])
        p_crossed = sb("p_crossed", [P, B, L])
        pT = sb("pT", [P, B, L])
        attn_hi = sb("attn_hi", [P, T], f32r)
        attn_lo = sb("attn_lo", [P, T], f32r)
        w_ffn = sb("w_ffn", [P, C * D])
        codes = sb("codes", [P, SLICE], i32)
        absmax = sb("absmax", [P, SLICE])
        scratch = sb("scratch", [P, 2 * SLICE])
        picked = scratch[:, 0:SLICE]
        level = scratch[:, SLICE:2 * SLICE]
        ident = sb("ident", [P, P])
        lnw = sb("lnw", [P, C])
        neg_max = sb("neg_max", [P, B])
        prob_sum = sb("prob_sum", [P, B])
        recip = sb("recip", [P, B])
        row_scale = sb("row_scale", [P, B])
        row_valid = sb("row_valid", [P, B])
        stats = sb("stats", [P, B, 6])
        mean_var = sb("mean_var", [P, B, 2])
        rstd = sb("rstd", [P, B])
        rms_a = sb("rms_a", [P, B])
        rms_b = sb("rms_b", [P, B])
        both = sb("both", [P, B])
        ln_shift = sb("ln_shift", [P, B])
        minus_half = sb("minus_half", [P, B])

        ctx_raw = v[:, :, :].rearrange("p b n -> p (b n)").rearrange("p (h c t) -> p h c t", h=2, c=C)
        mask_words = qk_raw[:, 1, 0:B * L // 4].bitcast(i32)
        mask_raw = mask_words.bitcast(u8).rearrange("p (b k) -> p b k", b=B)
        wa = p_crossed[0:R, 0:4, :].rearrange("p b k -> p (b k)")
        wb = p_crossed[0:R, 4:8, :].rearrange("p b k -> p (b k)")

        def tiles(t):
            flat = t.rearrange("p b k -> p (b k)")
            return [flat[:, i * D:(i + 1) * D] for i in range(2)]

        ffn_stage = tiles(p[:, :, :]) + tiles(pT[:, :, :])
        x_stage = ffn_stage + [qT[:, 0:D], qT[:, D:2 * D]] + tiles(p_crossed[:, :, :])

        proj_ps = [ctx.enter_context(nc.psum_tensor(f"proj_ps{i}", [P, D], f32)) for i in range(PROJ_BANKS)]
        out_ps = [ctx.enter_context(nc.psum_tensor(f"out_ps{i}", [P, D], f32)) for i in range(OUT_BANKS)]
        s_ps = [ctx.enter_context(nc.psum_tensor(f"s_ps{i}", [P, HB, L], f32)) for i in range(2)]

        ctx_loaded = [sem(f"ctx_loaded{i}") for i in range(C)]
        ctx_rest_loaded = sem("ctx_rest_loaded")
        keys_loaded = sem("keys_loaded")
        x_loaded = [sem(f"x_loaded{i}") for i in range(2)]
        mask_loaded = sem("mask_loaded")
        small_loaded = sem("small_loaded")
        qk_loaded = [sem(f"qk_loaded{i}") for i in range(2)]
        ob_loaded = [sem(f"ob_loaded{i}") for i in range(2)]
        wv_loaded = sem("wv_loaded")
        codes_loaded = sem("codes_loaded")
        stored = sem("stored")

        keys_hi_done = sem("keys_hi_done")
        keys_lo_done = sem("keys_lo_done")
        ctx_hi_done = sem("ctx_hi_done")
        ctx_lo_done = sem("ctx_lo_done")
        qk_hi_done = sem("qk_hi_done")
        qk_lo_done = sem("qk_lo_done")
        wo_hi_done = sem("wo_hi_done")
        wo_lo_done = sem("wo_lo_done")
        wv_hi_done = sem("wv_hi_done")
        wv_lo_done = sem("wv_lo_done")
        mask_done = sem("mask_done")
        bias_done = sem("bias_done")
        const_done = sem("const_done")

        proj_done = sem("proj_done")
        proj_drained = sem("proj_drained")
        out_done = sem("out_done")
        out_drained = sem("out_drained")
        scores_done = sem("scores_done")
        biased = sem("biased")
        max_done = sem("max_done")
        exp_done = sem("exp_done")
        recip_done = sem("recip_done")
        row_scale_done = sem("row_scale_done")
        p_done = sem("p_done")
        crossed = sem("crossed")
        turned = sem("turned")
        pT_done = sem("pT_done")
        attn_hi_done = sem("attn_hi_done")

        xT_hi_done = sem("xT_hi_done")
        stats_done = sem("stats_done")
        norm_step = sem("norm_step")
        norm_done = sem("norm_done")
        staged = sem("staged")
        hidden_step = sem("hidden_step")
        ident_step = sem("ident_step")
        decode_step = sem("decode_step")
        decoded = sem("decoded")
        pool_passed = sem("pool_passed")

        block = ctx.enter_context(nc.Block())

        @block.sync
        def _(sp):
            def load_qk(h, slot):
                sp.dma_start(qk_raw[:, slot, :], qk_d[h]).then_inc(qk_loaded[slot], 16)

            def load_ob(h, slot):
                sp.dma_start(ob_raw[:, slot, :], ob_d[h]).then_inc(ob_loaded[slot], 16)

            def load_wv(g):
                sp.dma_start(wv_raw[:, :, :].rearrange("p c n -> p (c n)"), wv_d[g]).then_inc(wv_loaded, 16)

            def load_codes(g):
                sp.dma_start(codes[:, :], codes_d[g]).then_inc(codes_loaded, 16)
                for s in range(2):
                    sp.dma_start(absmax[64 * s:64 * s + 64, :],
                                 absmax_d[g, s].partition_broadcast(64)).then_inc(codes_loaded, 16)

            keys = slice(C * DH, QK)
            sp.dma_start(qk_raw[:, 0, keys], qk_d[0, :, keys]).then_inc(keys_loaded, 16)
            for c in range(C):
                sp.dma_start(ctx_raw[:, 0, c, :], ctx_d[0, :, c]).then_inc(ctx_loaded[c], 16)
            sp.dma_start(lnw[:, :], lnw_d).then_inc(small_loaded, 16)
            sp.dma_start(wa, wa_d).then_inc(small_loaded, 16)
            sp.dma_start(wb, wb_d).then_inc(small_loaded, 16)
            load_wv(0)
            sp.dma_start(ctx_raw[:, 1, :, :], ctx_d[1]).then_inc(ctx_rest_loaded, 16)
            for hf in range(2):
                sp.dma_start(resid[:, hf * HB:(hf + 1) * HB, :],
                             x_d[hf * HB:(hf + 1) * HB].rearrange("b t d -> t b d")).then_inc(x_loaded[hf], 16)
            sp.dma_start(qk_raw[:, 0, 0:C * DH], qk_d[0, :, 0:C * DH]).then_inc(qk_loaded[0], 16)
            sp.dma_start(mask_words, mask_d).then_inc(mask_loaded, 16)
            load_ob(0, 0)
            load_ob(1, 1)
            load_codes(0)
            sp.wait_ge(mask_done, 2)
            load_qk(1, 1)
            for h in range(2):
                sp.wait_ge(qk_lo_done, h + 1)
                load_qk(h + 2, h)
            sp.wait_ge(wo_lo_done, 1)
            sp.wait_ge(bias_done, 1)
            load_ob(2, 0)

            def group(g, last):
                if not last:
                    sp.wait_ge(wv_lo_done, C * (g + 1))
                    load_wv(g + 1)
                for j in range(G):
                    h = G * g + j
                    if not (last and j + 4 >= G):
                        sp.wait_ge(qk_lo_done, h + 3)
                        load_qk(h + 4, j % 2)
                    if not (last and j + 3 >= G):
                        sp.wait_ge(wo_lo_done, h + 2)
                        sp.wait_ge(bias_done, h + 2)
                        load_ob(h + 3, (j + 1) % 2)
                if not last:
                    sp.wait_ge(decoded, g + 1)
                    load_codes(g + 1)

            with sp.Fori(0, GROUPS - 1) as g:
                group(g, False)
            group(GROUPS - 1, True)

            for b in range(B):
                sp.wait_ge(out_drained, OUT_BANKS + OUT_END + b + 1)
                sp.dma_start(out_d[b], resid[:, b, :]).then_inc(stored, 16)
            sp.wait_ge(stored, 16 * B)

        @block.gpsimd
        def _(pool):
            def passed(s, value):
                pool.wait_ge(s, value)
                pool.sem_inc(pool_passed, 1)

            pool.memset(minus_half[:, :], -0.5).then_inc(const_done, 1)
            pool.memset(ident[:, :], 0.0).then_inc(ident_step, 1)
            pool.wait_ge(ident_step, 1)
            pool.affine_select(out=ident[:, :], in_=ident[:, :], compare_op=ALU.not_equal, fill=1.0, base=0,
                               pattern=[[-1, P]], channel_multiplier=1).then_inc(const_done, 1)

            steps = [0]

            def norm(ins):
                ins.then_inc(norm_step, 1)
                steps[0] += 1
                pool.wait_ge(norm_step, steps[0])

            pool.wait_ge(const_done, 2)
            for hf in range(2):
                bs = slice(hf * HB, (hf + 1) * HB)
                var = mean_var[:, bs, 1]
                pool.wait_ge(stats_done, 2 * HB * (hf + 1))
                norm(pool.tensor_scalar(rms_a[:, bs], var, EPS, None, ALU.add))
                norm(pool.tensor_tensor(rstd[:, bs], rms_a[:, bs], minus_half[:, bs], ALU.pow))
                norm(pool.tensor_tensor(rms_a[:, bs], rstd[:, bs], rstd[:, bs], ALU.mult))
                norm(pool.tensor_tensor(rms_b[:, bs], rms_a[:, bs], var, ALU.mult))
                norm(pool.tensor_scalar(rms_a[:, bs], rms_b[:, bs], EPS, None, ALU.add))
                norm(pool.tensor_tensor(rms_b[:, bs], rms_a[:, bs], minus_half[:, bs], ALU.pow))
                pool.tensor_tensor(both[:, bs], rms_b[:, bs], rstd[:, bs], ALU.mult).then_inc(norm_done, 1)

            def make_bias(slot):
                pos = ob_raw[:, slot, D:OB].rearrange("p (o k) -> p o k", o=1).broadcast_to([P, B, L])
                pool.tensor_tensor(bias[:, :, :], pos, mask_add[:, :, :], ALU.add).then_inc(bias_done, 1)

            for b in range(B):
                if b == HB:
                    pool.wait_ge(mask_done, 2)
                    pool.wait_ge(ob_loaded[0], 16)
                    make_bias(0)
                pool.wait_ge(staged, b + 1)
                pool.tensor_scalar(scratch[:, :], resid[:, b, :], mean_var[:, b, 0:1], rstd[:, b:b + 1],
                                   ALU.subtract, ALU.mult).then_inc(hidden_step, 1)
                pool.wait_ge(hidden_step, 2 * b + 1)
                pool.tensor_tensor(resid[:, b, :], resid[:, b, :], scratch[:, :], ALU.add).then_inc(hidden_step, 1)
                pool.wait_ge(hidden_step, 2 * b + 2)

            per_slice = 2 * (len(NF4) - 1) + 1

            def decode(g, quarter):
                step = [per_slice * g + (0, 7, 13, 21)[quarter]]

                def then(ins):
                    ins.then_inc(decode_step, 1)
                    step[0] += 1
                    passed(decode_step, step[0])

                if quarter == 0:
                    passed(codes_loaded, 48 * (g + 1))
                for code in range(4 * quarter, 4 * quarter + 4):
                    value = NF4[code]
                    if value == 0.0:
                        continue
                    match = ALU.is_ge if code == len(NF4) - 1 else ALU.is_equal
                    then(pool.tensor_scalar(level if code == 0 else picked, codes[:, :], float(code), value,
                                            match, ALU.mult))
                    if code:
                        then(pool.tensor_tensor(level, level, picked, ALU.add))
                if quarter == 3:
                    then(pool.tensor_tensor(picked, level, absmax[:, :], ALU.mult))
                    at = bass.ds(g * SLICE, SLICE)
                    then(pool.tensor_tensor(w_ffn[:, at], w_ffn[:, at], picked, ALU.add))
                    pool.sem_inc(decoded, 1)

            def group(g, last):
                for j in range(G):
                    h = G * g + j
                    if not (last and j == G - 1):
                        passed(p_done, 2 * h + 2)
                        passed(ob_loaded[(j + 1) % 2], 16 * (2 * g + (j + 1) // 2 + 1))
                        make_bias((j + 1) % 2)
                    for quarter in (((0, 1), (2, 3), (), ())[j] if last else (j,)):
                        decode(g, quarter)
                    if last and j in (1, 2):
                        passed(wv_hi_done, C * GROUPS + j + 2)
                        pool.tensor_tensor(wv_lo[:, j + 1, :], w_ffn[:, (j + 1) * D:(j + 2) * D],
                                           wv_hi[:, j + 1, :].bitcast(f32), ALU.subtract).then_inc(wv_lo_done, 1)

            with pool.Fori(0, GROUPS - 1) as g:
                group(g, False)
            group(GROUPS - 1, True)

            for b in range(B):
                one = slice(b, b + 1)
                pool.wait_ge(stats_done, 2 * B + 2 * (b + 1))
                norm(pool.tensor_scalar(rms_a[:, one], mean_var[:, b, 1:2], EPS, None, ALU.add))
                norm(pool.tensor_tensor(rstd[:, one], rms_a[:, one], minus_half[:, one], ALU.pow))
                pool.tensor_scalar(ln_shift[:, one], mean_var[:, b, 0:1], rstd[:, one], -1.0,
                                   ALU.mult, ALU.mult).then_inc(norm_done, 1)

        @block.scalar
        def _(act):
            def copy(out, in_, **kw):
                return act.activation(out, in_, ACT.Copy, **kw)

            def split_wv(c, source):
                copy(wv_hi[:, c, :], source).then_inc(wv_hi_done, 1)

            def drain(n, bank, out, **kw):
                act.wait_ge(proj_done, n + 1)
                copy(out, proj_ps[bank][:, :], **kw).then_inc(proj_drained, 1)

            keys = slice(C * DH, QK)
            act.wait_ge(keys_loaded, 16)
            copy(qk_hi[:, 0, keys], qk_raw[:, 0, keys]).then_inc(keys_hi_done, 1)
            for c in range(C):
                act.wait_ge(ctx_loaded[c], 16)
                copy(ctx_hi[:, c, 0:HT], ctx_raw[:, 0, c, :]).then_inc(ctx_hi_done, 1)
            drain(0, 0, kT[:, 0:HT])

            def drain_lora(c):
                drain(1 + c, (1 + c) % 2, w_ffn[:, c * D:(c + 1) * D], scale=LORA_SCALE)

            for c in range(C):
                drain_lora(c)
                if c == 0:
                    act.wait_ge(wv_loaded, 16)
                split_wv(c, wv_raw[:, c, :])
            act.wait_ge(ctx_rest_loaded, 16)
            for c in range(C):
                copy(ctx_hi[:, c, HT:T], ctx_raw[:, 1, c, :]).then_inc(ctx_hi_done, 1)
            for b in range(HB):
                drain(1 + C + b, (1 + b) % 2, v[:, b, :])
            act.wait_ge(qk_loaded[0], 16)
            copy(qk_hi[:, 0, 0:C * DH], qk_raw[:, 0, 0:C * DH]).then_inc(qk_hi_done, 1)
            drain(1 + C + HB, 1, kT[:, HT:T])

            def xn_high(hf):
                for c in range(C):
                    act.wait_ge(out_done, C * hf + c + 1)
                    copy(xn_hi[:, c, hf * HT:(hf + 1) * HT], out_ps[c][:, :],
                         scale=lnw[:, c:c + 1]).then_inc(attn_hi_done, 1)

            act.wait_ge(small_loaded, 48)
            for b in range(HB, B):
                drain(2 + C + b, b % 2, v[:, b, :])
                if b == B - 2:
                    xn_high(0)
            xn_high(1)
            act.wait_ge(qk_loaded[1], 16)
            copy(qk_hi[:, 1, :], qk_raw[:, 1, :]).then_inc(qk_hi_done, 1)
            for hf in range(2):
                drain(B + C + 2 + hf, hf, qT[:, hf * HT:(hf + 1) * HT])
            act.wait_ge(ob_loaded[0], 16)
            copy(wo_hi[:, 0, :], ob_raw[:, 0, 0:D]).then_inc(wo_hi_done, 1)
            act.wait_ge(qk_loaded[0], 32)
            copy(qk_hi[:, 0, :], qk_raw[:, 0, :]).then_inc(qk_hi_done, 1)

            def exps(h, hf):
                act.wait_ge(max_done, 2 * h + hf + 1)
                for b in halves(hf):
                    e = act.activation(p[:, b, :], p[:, b, :], ACT.Exp, bias=neg_max[:, b:b + 1],
                                       accum_out=prob_sum[:, b:b + 1])
                e.then_inc(exp_done, 1)

            def group(g, last):
                for j in range(G):
                    h = G * g + j
                    final = last and j == G - 1
                    n = PROJ_FIRST + PROJ_GROUP * g + 4 * j
                    if not final:
                        for hf in range(2):
                            drain(n + hf, hf, qT[:, hf * HT:(hf + 1) * HT])
                        slot = (j + 1) % 2
                        act.wait_ge(ob_loaded[slot], 16 * (2 * g + (j + 1) // 2 + 1))
                        act.wait_ge(out_done, OUT_FIRST + OUT_HEAD * h)
                        copy(wo_hi[:, slot, :], ob_raw[:, slot, 0:D]).then_inc(wo_hi_done, 1)
                        for hf in range(2):
                            drain(n + 2 + hf, hf, kT[:, hf * HT:(hf + 1) * HT])
                    else:
                        for hf in range(2):
                            act.wait_ge(turned, hf + 1)
                            copy(pT[:, hf * HB:(hf + 1) * HB, :], s_ps[hf][:, :, :]).then_inc(pT_done, 1)
                    for hf in range(2):
                        act.wait_ge(out_done, OUT_FIRST + OUT_HEAD * h + hf + 1)
                        copy(attn_hi[:, hf * HT:(hf + 1) * HT],
                             out_ps[(2 * j + hf) % OUT_BANKS][:, :]).then_inc(attn_hi_done, 1)
                    if not (last and j + 3 >= G):
                        slot = (j + 1) % 2
                        act.wait_ge(qk_loaded[slot], 16 * (2 * g + (j + 3) // 2 + 1))
                        copy(qk_hi[:, slot, :], qk_raw[:, slot, :]).then_inc(qk_hi_done, 1)
                    if not last:
                        if j == 0:
                            act.wait_ge(wv_loaded, 16 * (g + 2))
                        for c in ((0, 1), (2,), (3,), ())[j]:
                            split_wv(c, wv_raw[:, c, :])
                        for hf in range(2):
                            exps(h + 1, hf)
                    elif not final:
                        if j < 2:
                            act.wait_ge(decoded, GROUPS - 1)
                            for c in ((0,), (1, 2))[j]:
                                split_wv(c, w_ffn[:, c * D:(c + 1) * D])
                        exps(h + 1, 0)
                        if j == 2:
                            act.wait_ge(decoded, GROUPS)
                            split_wv(C - 1, w_ffn[:, (C - 1) * D:C * D])
                        exps(h + 1, 1)
                    if not last and j == G - 1:
                        for b in range(B):
                            drain(n + 4 + b, b % 2, v[:, b, :])

            for hf in range(2):
                exps(0, hf)
            with act.Fori(0, GROUPS - 1) as g:
                group(g, False)
            group(GROUPS - 1, True)

            def ffn_norm(b):
                act.wait_ge(norm_done, 2 + b + 1)
                if b >= 4:
                    act.wait_ge(proj_done, PROJ_END + b - 4 + 1)
                act.activation(ffn_stage[b % 4], resid[:, b, :], ACT.Identity, bias=ln_shift[:, b:b + 1],
                               scale=rstd[:, b:b + 1]).then_inc(staged, 1)

            ffn_norm(0)
            ffn_norm(1)
            for b in range(B):
                if b in range(2, B - 1):
                    ffn_norm(b + 1)
                act.wait_ge(proj_done, PROJ_END + b + 1)
                copy(xn_hi[:, :, b * L:(b + 1) * L],
                     proj_ps[b % 2][:, :].rearrange("p (c t) -> p c t", c=C)).then_inc(xT_hi_done, 1)
                if b == 1:
                    ffn_norm(2)

        @block.vector
        def _(dve):
            def lo(out, whole, hi):
                return dve.tensor_tensor(out, whole, hi.bitcast(f32), ALU.subtract)

            def out_count(h):
                return OUT_FIRST + OUT_HEAD * h

            dve.memset(neg_max[:, :], 0.0).then_inc(out_drained, OUT_BANKS)

            def tile_stats(b, before):
                dve.bn_stats(stats[:, b, :], resid[:, b, :]).then_inc(stats_done, 1)
                dve.wait_ge(stats_done, before + 1)
                dve.bn_aggr(mean_var[:, b, :], stats[:, b, :]).then_inc(stats_done, 1)

            keys = slice(C * DH, QK)
            dve.wait_ge(keys_hi_done, 1)
            lo(qk_lo[:, 0, keys], qk_raw[:, 0, keys], qk_hi[:, 0, keys]).then_inc(keys_lo_done, 1)
            for c in range(C):
                dve.wait_ge(ctx_hi_done, c + 1)
                lo(ctx_lo[:, c, 0:HT], ctx_raw[:, 0, c, :], ctx_hi[:, c, 0:HT]).then_inc(ctx_lo_done, 1)
            for c in range(C):
                dve.wait_ge(wv_hi_done, c + 1)
                lo(wv_lo[:, c, :], wv_raw[:, c, :], wv_hi[:, c, :]).then_inc(wv_lo_done, 1)
            for c in range(C):
                dve.wait_ge(ctx_hi_done, C + c + 1)
                lo(ctx_lo[:, c, HT:T], ctx_raw[:, 1, c, :], ctx_hi[:, c, HT:T]).then_inc(ctx_lo_done, 1)
            for hf in range(2):
                dve.wait_ge(x_loaded[hf], 16)
                for b in halves(hf):
                    tile_stats(b, 2 * b)
            dve.wait_ge(proj_done, 1 + C)
            for hf in range(2):
                dve.wait_ge(norm_done, hf + 1)
                for b in halves(hf):
                    dve.tensor_scalar(x_stage[b], resid[:, b, :], mean_var[:, b, 0:1], both[:, b:b + 1],
                                      ALU.subtract, ALU.mult).then_inc(staged, 1)
            dve.wait_ge(qk_hi_done, 1)
            lo(qk_lo[:, 0, 0:C * DH], qk_raw[:, 0, 0:C * DH], qk_hi[:, 0, 0:C * DH]).then_inc(qk_lo_done, 1)
            dve.wait_ge(mask_loaded, 16)
            dve.tensor_scalar(mask_add[:, :, :], mask_raw, 1.0, -MASKED, ALU.subtract, ALU.mult).then_inc(mask_done, 1)
            dve.tensor_reduce(row_valid[:, :], mask_raw, AX.X, ALU.max).then_inc(mask_done, 1)

            for hf in range(2):
                for c in range(C):
                    dve.wait_ge(attn_hi_done, C * hf + c + 1)
                    dve.scalar_tensor_tensor(
                        xn_lo[:, c, hf * HT:(hf + 1) * HT], out_ps[c][:, :], lnw[:, c:c + 1],
                        xn_hi[:, c, hf * HT:(hf + 1) * HT].bitcast(f32), ALU.mult, ALU.subtract,
                    ).then_inc(out_drained, 1)
            dve.wait_ge(qk_hi_done, 2)
            lo(qk_lo[:, 1, :], qk_raw[:, 1, :], qk_hi[:, 1, :]).then_inc(qk_lo_done, 1)
            dve.wait_ge(wo_hi_done, 1)
            lo(wo_lo[:, 0, :], ob_raw[:, 0, 0:D], wo_hi[:, 0, :]).then_inc(wo_lo_done, 1)

            def bias_and_max(h, hf):
                bs = slice(hf * HB, (hf + 1) * HB)
                dve.wait_ge(scores_done, 2 * h + hf + 1)
                if hf == 0:
                    dve.wait_ge(bias_done, h + 1)
                dve.tensor_tensor(p[:, bs, :], s_ps[hf][:, :, :], bias[:, bs, :], ALU.add).then_inc(biased, 1)
                dve.wait_ge(biased, 2 * h + hf + 1)
                dve.tensor_reduce(neg_max[:, bs], p[:, bs, :], AX.X, ALU.max, negate=True).then_inc(max_done, 1)

            def normalise(h, hf):
                bs = slice(hf * HB, (hf + 1) * HB)
                dve.wait_ge(exp_done, 2 * h + hf + 1)
                dve.reciprocal(recip[:, bs], prob_sum[:, bs]).then_inc(recip_done, 1)
                dve.wait_ge(recip_done, 2 * h + hf + 1)
                dve.tensor_tensor(row_scale[:, bs], recip[:, bs], row_valid[:, bs],
                                  ALU.mult).then_inc(row_scale_done, 1)
                dve.wait_ge(row_scale_done, 2 * h + hf + 1)
                scale = row_scale[:, bs].rearrange("p (b o) -> p b o", o=1).broadcast_to([P, HB, L])
                dve.tensor_tensor(p[:, bs, :], p[:, bs, :], scale, ALU.mult).then_inc(p_done, 1)

            def cross_and_transpose(h):
                dve.wait_ge(p_done, 2 * h + 2)
                for i in range(P // Q):
                    for k in range(P // Q):
                        a, b = slice(Q * i, Q * (i + 1)), slice(Q * k, Q * (k + 1))
                        e = dve.tensor_copy(p_crossed[b, :, a], p[a, :, b])
                e.then_inc(crossed, 1)
                dve.wait_ge(crossed, h + 1)
                for hf in range(2):
                    bs = slice(hf * HB, (hf + 1) * HB)
                    dve.transpose(pT[:, bs, :].rearrange("p b q -> p (b q)"),
                                  p_crossed[:, bs, :].rearrange("p b q -> p (b q)")).then_inc(pT_done, 1)

            def xT_low(b):
                dve.wait_ge(xT_hi_done, b + 1)
                at = slice(b * L, (b + 1) * L)
                lo(xn_lo[:, :, at], proj_ps[b % 2][:, :].rearrange("p (c t) -> p c t", c=C),
                   xn_hi[:, :, at]).then_inc(proj_drained, 1)

            def add(b, bank):
                dve.tensor_tensor(resid[:, b, :], out_ps[bank][:, :], resid[:, b, :], ALU.add).then_inc(out_drained, 1)

            def ffn_stats(b):
                dve.wait_ge(out_drained, OUT_BANKS + OUT_END - B + b + 1)
                tile_stats(b, 2 * B + 2 * b)

            def group(g, last):
                for j in range(G):
                    h = G * g + j
                    final = last and j == G - 1
                    hurry = last and j == G - 2
                    if not final:
                        for hf in range(2):
                            normalise(h, hf)
                        cross_and_transpose(h)
                    if not (last and j + 2 >= G):
                        slot = j % 2
                        dve.wait_ge(qk_hi_done, h + 3)
                        lo(qk_lo[:, slot, :], qk_raw[:, slot, :], qk_hi[:, slot, :]).then_inc(qk_lo_done, 1)
                    if not final:
                        slot = (j + 1) % 2
                        dve.wait_ge(wo_hi_done, h + 2)
                        lo(wo_lo[:, slot, :], ob_raw[:, slot, 0:D], wo_hi[:, slot, :]).then_inc(wo_lo_done, 1)
                    if hurry:
                        bias_and_max(h + 1, 0)
                    for hf in range(2):
                        dve.wait_ge(attn_hi_done, 2 * C + 2 * h + hf + 1)
                        at = slice(hf * HT, (hf + 1) * HT)
                        lo(attn_lo[:, at], out_ps[(2 * j + hf) % OUT_BANKS][:, :],
                           attn_hi[:, at]).then_inc(out_drained, 1)
                    if hurry:
                        bias_and_max(h + 1, 1)
                    if last and j < 2:
                        dve.wait_ge(wv_hi_done, C * GROUPS + j + 1)
                        lo(wv_lo[:, j, :], w_ffn[:, j * D:(j + 1) * D], wv_hi[:, j, :]).then_inc(wv_lo_done, 1)
                    for b in range(B):
                        dve.wait_ge(out_done, out_count(h) + 2 + b + 1)
                        if b == 0:
                            dve.wait_ge(hidden_step, 2 * B)
                            dve.wait_ge(out_drained, OUT_BANKS + out_count(h) + 2)
                        add(b, (2 * j + 2 + b) % OUT_BANKS)
                        if hurry and b in NORMALISE_AFTER:
                            normalise(h + 1, NORMALISE_AFTER.index(b))
                        if b == HB - 1 and not (hurry or final):
                            for hf in range(2):
                                bias_and_max(h + 1, hf)
                        if final:
                            for t in ((0,), (1,), (), (2,), (), (), (), ())[b]:
                                ffn_stats(t)
                            for t in ((), (), (), (0,), (1,), (), (2,), ())[b]:
                                xT_low(t)
                            for t in ((), (), (), (), (3,), (4,), (5,), ())[b]:
                                ffn_stats(t)
                    if not last:
                        for c in ((0, 1), (2,), (3,), ())[j]:
                            dve.wait_ge(wv_hi_done, C * (g + 1) + c + 1)
                            lo(wv_lo[:, c, :], wv_raw[:, c, :], wv_hi[:, c, :]).then_inc(wv_lo_done, 1)

            for hf in range(2):
                bias_and_max(0, hf)
            with dve.Fori(0, GROUPS - 1) as g:
                group(g, False)
            group(GROUPS - 1, True)

            for b in range(B):
                dve.wait_ge(out_done, OUT_END + b + 1)
                add(b, b % OUT_BANKS)
                if b < 2:
                    ffn_stats(b + 6)
                if b + 3 < B:
                    xT_low(b + 3)

        @block.tensor
        def _(pe):
            def three(out, pairs, sem_done, wait=None):
                n = 3 * len(pairs)
                i = 0
                for c, ((l_hi, l_lo), (r_hi, r_lo)) in enumerate(pairs):
                    if wait:
                        wait(c)
                    for l, r in ((l_hi, r_hi), (l_hi, r_lo), (l_lo, r_hi)):
                        m = pe.matmul(out, l, r, start=(i == 0), stop=(i == n - 1))
                        i += 1
                m.then_inc(sem_done, 1)

            def proj_bank(n, bank):
                pe.wait_ge(proj_drained, n - PROJ_BANKS + 1)
                return proj_ps[bank][:, :]

            def value_pairs(b):
                at = slice(b * L, (b + 1) * L)
                return [((ctx_hi[:, c, at], ctx_lo[:, c, at]), (wv_hi[:, c, :], wv_lo[:, c, :])) for c in range(C)]

            def values(n, bank, b):
                three(proj_bank(n, bank), value_pairs(b), proj_done)

            def project(n, slot, which, hf):
                a_hi, a_lo = ((xn_hi, xn_lo), (ctx_hi, ctx_lo))[which]
                at = slice(hf * HT, (hf + 1) * HT)

                def w(t, c):
                    k = (which * C + c) * DH
                    return t[:, slot, k:k + DH]

                three(proj_bank(n, hf),
                      [((w(qk_hi, c), w(qk_lo, c)), (a_hi[:, c, at], a_lo[:, c, at])) for c in range(C)],
                      proj_done)

            def first_keys():
                w = [slice((C + c) * DH, (C + c + 1) * DH) for c in range(C)]
                three(proj_ps[0][:, :],
                      [((qk_hi[:, 0, w[c]], qk_lo[:, 0, w[c]]), (ctx_hi[:, c, 0:HT], ctx_lo[:, c, 0:HT]))
                       for c in range(C)], proj_done, wait=lambda c: pe.wait_ge(ctx_lo_done, c + 1))

            def scores(h, hf, n, first=False):
                pe.wait_ge(proj_drained, n - 1 + hf)
                if not first:
                    pe.wait_ge(biased, 2 * h)
                for i, b in enumerate(halves(hf)):
                    at = slice(b * L, (b + 1) * L)
                    s = pe.matmul(s_ps[hf][:, i, :], qT[:, at], kT[:, at], start=True, stop=True)
                s.then_inc(scores_done, 1)

            def turn(hf):
                pe.wait_ge(p_done, 2 * (H - 1) + hf + 1)
                for i, b in enumerate(halves(hf)):
                    t = pe.transpose(s_ps[hf][:, i, :], p[:, b, :], ident[:, :])
                t.then_inc(turned, 1)

            def ffn_transpose(b):
                pe.wait_ge(staged, B + b + 1)
                bank = proj_bank(PROJ_END + b, b % 2)
                for c in range(C):
                    t = pe.transpose(bank[:, c * P:(c + 1) * P], ffn_stage[b % 4][:, c * P:(c + 1) * P], ident[:, :])
                t.then_inc(proj_done, 1)

            def out_bank(n_bank, count):
                pe.wait_ge(out_drained, count)
                return out_ps[n_bank]

            pe.wait_ge(const_done, 2)
            for _ in range(WARM_UP):
                pe.matmul(proj_ps[0][:, 0:P], ident[:, :], ident[:, :], start=True, stop=True)

            pe.wait_ge(keys_lo_done, 1)
            first_keys()
            pe.wait_ge(small_loaded, 48)
            for c in range(C):
                bank = proj_ps[1][:, :] if c == 0 else proj_bank(1 + c, (1 + c) % 2)
                pe.matmul(bank, wa[:, c * P:(c + 1) * P], wb, start=True, stop=True).then_inc(proj_done, 1)
            three(proj_bank(1 + C, 1), value_pairs(0), proj_done, wait=lambda c: pe.wait_ge(wv_lo_done, c + 1))
            for b in range(1, HB):
                values(1 + C + b, (1 + b) % 2, b)
            pe.wait_ge(ctx_lo_done, 2 * C)
            project(1 + C + HB, 0, 1, 1)

            def transpose_x(hf):
                pe.wait_ge(staged, HB * (hf + 1))
                for c in range(C):
                    bank = out_bank(c, C * hf + c + 1)
                    for i, b in enumerate(halves(hf)):
                        t = pe.transpose(bank[:, i * P:(i + 1) * P], x_stage[b][:, c * P:(c + 1) * P], ident[:, :])
                    t.then_inc(out_done, 1)

            for b in range(HB, B):
                values(2 + C + b, b % 2, b)
                if b == B - 2:
                    transpose_x(0)
            transpose_x(1)
            pe.wait_ge(qk_lo_done, 1)
            for hf in range(2):
                pe.wait_ge(out_drained, OUT_BANKS + C * (hf + 1))
                project(B + C + 2 + hf, 0, 0, hf)

            def group(g, last):
                for j in range(G):
                    h = G * g + j
                    final = last and j == G - 1
                    hurry = last and j == G - 2
                    n = PROJ_FIRST + PROJ_GROUP * g + 4 * j
                    m = OUT_FIRST + OUT_HEAD * h
                    if not final:
                        slot = (j + 1) % 2
                        pe.wait_ge(qk_lo_done, h + 2)
                        for k in range(4):
                            project(n + k, slot, k // 2, k % 2)
                    if hurry:
                        scores(h + 1, 0, n + 4)
                    for hf in range(2):
                        pe.wait_ge(pT_done, 2 * h + hf + 1)
                        bank = out_bank((2 * j + hf) % OUT_BANKS, m + hf + 1)
                        for i, b in enumerate(halves(hf)):
                            o = pe.matmul(bank[:, i * L:(i + 1) * L], v[:, b, j * DH:(j + 1) * DH], pT[:, b, :],
                                          start=True, stop=True)
                        o.then_inc(out_done, 1)
                    if not final:
                        for hf in range(1 if hurry else 0, 2):
                            scores(h + 1, hf, n + 4)
                    pe.wait_ge(wo_lo_done, h + 1)
                    for b in range(B):
                        if b % HB == 0:
                            pe.wait_ge(out_drained, OUT_BANKS + m + b // HB + 1)
                        if hurry and b in TURN_BEFORE:
                            turn(TURN_BEFORE.index(b))
                        if final and b == FFN_TRANSPOSE_BEFORE:
                            ffn_transpose(0)
                        at = slice(b * L, (b + 1) * L)
                        bank = out_bank((2 * j + 2 + b) % OUT_BANKS, m + 2 + b + 1)
                        three(bank[:, :], [((attn_hi[:, at], attn_lo[:, at]), (wo_hi[:, j % 2, :], wo_lo[:, j % 2, :]))],
                              out_done)
                    if not last and j == G - 1:
                        pe.wait_ge(wv_lo_done, C * (g + 2))
                        for b in range(B):
                            values(n + 4 + b, b % 2, b)

            for hf in range(2):
                scores(0, hf, B + C + 4, first=True)
            with pe.Fori(0, GROUPS - 1) as g:
                group(g, False)
            group(GROUPS - 1, True)

            def ffn_product(b):
                at = slice(b * L, (b + 1) * L)
                pe.wait_ge(proj_drained, PROJ_END + b + 1)
                bank = out_bank(b % OUT_BANKS, OUT_END + b + 1)
                three(bank[:, :], [((xn_hi[:, c, at], xn_lo[:, c, at]), (wv_hi[:, c, :], wv_lo[:, c, :]))
                                   for c in range(C)], out_done)

            for b in range(B):
                if b + 1 < B:
                    ffn_transpose(b + 1)
                if b == 0:
                    pe.wait_ge(wv_lo_done, C * (GROUPS + 1))
                ffn_product(b)


def kernel(x, ctx_4096, mask_BxSxS2_bk0, L0_xattn_position_bias, L0_xattn_ln_weight, L0_xattn_w_q, L0_xattn_w_k,
           L0_xattn_w_v, L0_xattn_w_out, L0_ffn_w_codes, L0_ffn_absmax, L0_ffn_W_a, L0_ffn_W_b):
    import concourse.bacc as bacc
    from concourse.bass_utils import run_bass_kernel_spmd

    def head_weights(w):
        return np.asarray(w).reshape(H, DH, C, P).transpose(0, 3, 2, 1).reshape(H, P, C * DH)

    tokens_last = np.asarray(ctx_4096).reshape(2, HT, C, P).transpose(0, 3, 2, 1)
    wo = np.asarray(L0_xattn_w_out).reshape(D, H, DH).transpose(1, 2, 0)
    pos = np.asarray(L0_xattn_position_bias)
    wv = np.asarray(L0_xattn_w_v).reshape(GROUPS, G * DH, C, P).transpose(0, 3, 2, 1)
    codes = np.asarray(L0_ffn_w_codes).T.reshape(C, P, 2, SLICE).transpose(0, 2, 1, 3)
    absmax = np.asarray(L0_ffn_absmax).T.reshape(C, 2, 2, SLICE).transpose(0, 2, 1, 3)
    mask = np.ascontiguousarray(np.asarray(mask_BxSxS2_bk0).transpose(1, 0, 2)).reshape(L, B * L)
    data = {
        "x_dram": np.asarray(x),
        "ctx_dram": tokens_last,
        "mask_dram": mask.view(np.int32),
        "lnw_dram": np.asarray(L0_xattn_ln_weight).reshape(C, P).T,
        "qk_dram": np.concatenate([head_weights(L0_xattn_w_q), head_weights(L0_xattn_w_k)], axis=2),
        "ob_dram": np.concatenate([wo, pos], axis=2),
        "wv_dram": wv.reshape(GROUPS, P, C * G * DH),
        "codes_dram": codes.reshape(GROUPS, P, SLICE),
        "absmax_dram": absmax.reshape(GROUPS, 2, SLICE),
        "wa_dram": np.asarray(L0_ffn_W_a).T,
        "wb_dram": np.asarray(L0_ffn_W_b),
    }
    data = {name: np.ascontiguousarray(a) for name, a in data.items()}
    nc = bacc.Bacc("TRN2", target_bir_lowering=False, num_devices=1)
    ins = [nc.dram_tensor(name, a.shape, mybir.dt.from_np(a.dtype), kind="ExternalInput").ap()
           for name, a in data.items()]
    out = nc.dram_tensor("out_dram", (B, L, D), f32, kind="ExternalOutput").ap()
    xattn_ffn(nc, *ins, out)
    r = run_bass_kernel_spmd(nc, [data], core_ids=[0])
    return r.results[0]["out_dram"]
```
